# Optimizing a Trainium2 kernel written in Bass

```python
import numpy as np
import jax
import jax.numpy as jnp

def _softmax(x, axis=-1):
    return jax.nn.softmax(x, axis=axis)

def _gelu(x):
    return jax.nn.gelu(x, approximate=True)

def _silu(x):
    return jax.nn.silu(x)

def _sigmoid(x):
    return jax.nn.sigmoid(x)

def _layernorm(x, axis=-1, eps=1e-05):
    m = jnp.mean(x, axis=axis, keepdims=True)
    v = jnp.var(x, axis=axis, keepdims=True)
    return (x - m) / jnp.sqrt(v + eps)

def _scatter_add(tgt, idx, src, axis=0):
    return tgt.at[idx].add(src)

def _segment_sum(src, seg, n):
    return jax.ops.segment_sum(src, seg, n)
kernel_name = 'mk_cond_resid_d4_seqx_r4_aa3ea5'

def setup_inputs(seed: int=0):
    np.random.seed(seed)
    _w = jnp.asarray

    def _rec_inputs():
        import jax
        import jax.numpy as jnp
        _rk = jax.random.key(seed)
        x = 7.22e-05 + 1 * jax.random.normal(jax.random.fold_in(_rk, 1), (32, 256, 256), jnp.float32)
        _lenS = 256 - jax.random.randint(jax.random.fold_in(_rk, 7), (32,), 0, max(1, 256 // 4) + 1, jnp.int32)
        _lenS2 = 256 - jax.random.randint(jax.random.fold_in(_rk, 8), (32,), 0, max(1, 256 // 4) + 1, jnp.int32)
        fside_BxSxS_0 = 4.13588e-05 + 0.999923 * jax.random.normal(jax.random.fold_in(_rk, 11), (32, 256, 256), jnp.float32)
        itok_B_18_1004 = jax.random.randint(jax.random.fold_in(_rk, 12), (32,), 18, 1005, jnp.int32)
        itok_B_0_8 = jax.random.randint(jax.random.fold_in(_rk, 13), (32,), 0, 9, jnp.int32)
        itok_B_0_7 = jax.random.randint(jax.random.fold_in(_rk, 14), (32,), 0, 8, jnp.int32)
        itok_B_0_2 = jax.random.randint(jax.random.fold_in(_rk, 15), (32,), 0, 3, jnp.int32)
        return (x, fside_BxSxS_0, itok_B_18_1004, itok_B_0_8, itok_B_0_7, itok_B_0_2)
    x, fside_BxSxS_0, itok_B_18_1004, itok_B_0_8, itok_B_0_7, itok_B_0_2 = _rec_inputs()

    def _L0_cond_setup():
        import jax, jax.numpy as jnp
        import numpy as np
        B, L1, L2, DIN, DOUT, H = (8, 256, 256, 256, 256, 16)
        DH = DOUT // H
        SCALE = 1.0 / np.sqrt(DH).astype(np.float32)
        key = jax.random.key(seed)
        ks = jax.random.split(key, 13)
        s = 0.02
        return {'seq1': jax.random.normal(ks[0], (B, L1, DIN), jnp.float32), 'seq2': jax.random.normal(ks[1], (B, L2, DIN), jnp.float32), 'seq_len1': jax.random.randint(ks[2], (B,), 1, L1 + 1, jnp.int32), 'Wq': jax.random.normal(ks[3], (DIN, DOUT), jnp.float32) * s, 'bq': jnp.zeros((DOUT,), jnp.float32), 'Wk': jax.random.normal(ks[4], (DIN, DOUT), jnp.float32) * s, 'bk': jnp.zeros((DOUT,), jnp.float32), 'Wv': jax.random.normal(ks[5], (DIN, DOUT), jnp.float32) * s, 'bv': jnp.zeros((DOUT,), jnp.float32), 'Wo': jax.random.normal(ks[6], (DOUT, DOUT), jnp.float32) * s, 'bo': jnp.zeros((DOUT,), jnp.float32), 'b_prev': jax.random.normal(ks[7], (1, 1, DIN), jnp.float32) * s, 'b_self': jax.random.normal(ks[8], (1, 1, DIN), jnp.float32) * s}
    _L0_cond_all = _L0_cond_setup()
    _L0_cond_in = {k: v for k, v in _L0_cond_all.items() if k in ('Wq', 'bq', 'Wk', 'bk', 'Wv', 'bv', 'Wo', 'bo', 'b_prev', 'b_self')}
    del _L0_cond_all

    def _L1_cond_setup():
        import jax, jax.numpy as jnp
        import numpy as np
        LN_EPS = 1e-05
        key = jax.random.key(seed)
        ks = jax.random.split(key, 8)
        B, S, H, A, L = (32, 512, 256, 64, 10)
        return {'hidden_states': jax.random.normal(ks[0], (B, S, H), dtype=jnp.float32), 'language_ids': jax.random.randint(ks[1], (B,), 0, L, dtype=jnp.int64), 'W1': jax.random.normal(ks[2], (L, H, A), dtype=jnp.float32) * (1.0 / np.sqrt(H)), 'b1': jnp.zeros((L, A), dtype=jnp.float32), 'W2': jax.random.normal(ks[3], (L, A, H), dtype=jnp.float32) * (1.0 / np.sqrt(A)), 'b2': jnp.zeros((L, H), dtype=jnp.float32), 'gamma': jnp.ones((L, H), dtype=jnp.float32), 'beta': jnp.zeros((L, H), dtype=jnp.float32)}
    _L1_cond_all = _L1_cond_setup()
    _L1_cond_in = {k: v for k, v in _L1_cond_all.items() if k in ('W1', 'b1', 'W2', 'b2', 'gamma', 'beta')}
    del _L1_cond_all

    def _L2_cond_setup():
        import jax, jax.numpy as jnp
        import numpy as np
        S, O, H = (8, 256, 256)
        B, N = (32, 128)
        key = jax.random.key(seed)
        k1, k2, k3, k4 = jax.random.split(key, 4)
        x = jax.random.normal(k1, (B, N, H), dtype=jnp.float32)
        subject_id = jax.random.randint(k2, (B,), 0, S)
        wbound = jnp.sqrt(2.0 / 6.0) * jnp.sqrt(3.0 / H)
        weight = jax.random.uniform(k3, (S, O, H), minval=-wbound, maxval=wbound, dtype=jnp.float32)
        bbound = 1.0 / jnp.sqrt(H)
        bias = jax.random.uniform(k4, (S, O), minval=-bbound, maxval=bbound, dtype=jnp.float32)
        return {'x': x, 'subject_id': subject_id, 'weight': weight, 'bias': bias}
    _L2_cond_all = _L2_cond_setup()
    _L2_cond_in = {k: v for k, v in _L2_cond_all.items() if k in ('weight', 'bias')}
    del _L2_cond_all

    def _L3_cond_setup():
        import jax, jax.numpy as jnp
        import numpy as np
        NEG_INF = -1e+30
        key = jax.random.key(seed)
        k1, k2, k3, k4, k5 = jax.random.split(key, 5)
        B, S, D, A = (16, 256, 256, 64)
        hidden = jax.random.normal(k1, (B, S, D), dtype=jnp.float32)
        W1 = jax.random.normal(k2, (D, A), dtype=jnp.float32) / np.sqrt(D)
        b1 = jax.random.normal(k3, (A,), dtype=jnp.float32) * 0.01
        v = jax.random.normal(k4, (A,), dtype=jnp.float32) / np.sqrt(A)
        prompt_type_ids = jax.random.randint(k5, (B,), 0, 3, dtype=jnp.int32)
        return {'hidden': hidden, 'W1': W1, 'b1': b1, 'v': v, 'prompt_type_ids': prompt_type_ids}
    _L3_cond_all = _L3_cond_setup()
    _L3_cond_in = {k: v for k, v in _L3_cond_all.items() if k in ('W1', 'b1', 'v')}
    del _L3_cond_all
    return {'x': x, 'fside_BxSxS_0': fside_BxSxS_0, 'itok_B_18_1004': itok_B_18_1004, 'itok_B_0_8': itok_B_0_8, 'itok_B_0_7': itok_B_0_7, 'itok_B_0_2': itok_B_0_2, 'L0_cond_Wq': _L0_cond_in['Wq'], 'L0_cond_bq': _L0_cond_in['bq'], 'L0_cond_Wk': _L0_cond_in['Wk'], 'L0_cond_bk': _L0_cond_in['bk'], 'L0_cond_Wv': _L0_cond_in['Wv'], 'L0_cond_bv': _L0_cond_in['bv'], 'L0_cond_Wo': _L0_cond_in['Wo'], 'L0_cond_bo': _L0_cond_in['bo'], 'L0_cond_b_prev': _L0_cond_in['b_prev'], 'L0_cond_b_self': _L0_cond_in['b_self'], 'L1_cond_W1': _L1_cond_in['W1'], 'L1_cond_b1': _L1_cond_in['b1'], 'L1_cond_W2': _L1_cond_in['W2'], 'L1_cond_b2': _L1_cond_in['b2'], 'L1_cond_gamma': _L1_cond_in['gamma'], 'L1_cond_beta': _L1_cond_in['beta'], 'L2_cond_weight': _L2_cond_in['weight'], 'L2_cond_bias': _L2_cond_in['bias'], 'L3_cond_W1': _L3_cond_in['W1'], 'L3_cond_b1': _L3_cond_in['b1'], 'L3_cond_v': _L3_cond_in['v']}

def reference(x, fside_BxSxS_0, itok_B_18_1004, itok_B_0_8, itok_B_0_7, itok_B_0_2, L0_cond_Wq, L0_cond_bq, L0_cond_Wk, L0_cond_bk, L0_cond_Wv, L0_cond_bv, L0_cond_Wo, L0_cond_bo, L0_cond_b_prev, L0_cond_b_self, L1_cond_W1, L1_cond_b1, L1_cond_W2, L1_cond_b2, L1_cond_gamma, L1_cond_beta, L2_cond_weight, L2_cond_bias, L3_cond_W1, L3_cond_b1, L3_cond_v):
    import jax
    import jax.numpy as jnp

    def _L0_cond_ref(seq1, seq2, seq_len1, Wq, bq, Wk, bk, Wv, bv, Wo, bo, b_prev, b_self):
        import jax, jax.numpy as jnp
        import numpy as np
        B, L1, L2, DIN, DOUT, H = (8, 256, 256, 256, 256, 16)
        DH = DOUT // H
        SCALE = 1.0 / np.sqrt(DH).astype(np.float32)
        b, l1, _ = seq1.shape
        l2 = seq2.shape[1]
        query = seq2 + b_self
        key = jnp.concatenate([seq1 + b_prev, seq2 + b_self], 1)
        value = jnp.concatenate([seq1, seq2], 1)
        q = (query @ Wq + bq).reshape(b, l2, H, DH).transpose(0, 2, 1, 3)
        k = (key @ Wk + bk).reshape(b, l1 + l2, H, DH).transpose(0, 2, 1, 3)
        v = (value @ Wv + bv).reshape(b, l1 + l2, H, DH).transpose(0, 2, 1, 3)
        score_prev = jnp.einsum('bhqd,bhkd->bhqk', q, k[:, :, :l1]) * SCALE
        score_self = (q * k[:, :, l1:]).sum(-1, keepdims=True) * SCALE
        mask = jnp.arange(l1)[None, :] < seq_len1[:, None]
        score_prev = jnp.where(mask[:, None, None, :], score_prev, -jnp.inf)
        score = jnp.concatenate([score_prev, score_self], -1)
        weights = jax.nn.softmax(score, axis=-1)
        attn = jnp.einsum('bhqk,bhkd->bhqd', weights[..., :-1], v[:, :, :l1])
        attn = attn + weights[..., -1:] * v[:, :, l1:]
        attn = attn.transpose(0, 2, 1, 3).reshape(b, l2, H * DH)
        return attn @ Wo + bo

    def _L1_cond_ref(hidden_states, language_ids, W1, b1, W2, b2, gamma, beta):
        import jax, jax.numpy as jnp
        import numpy as np
        LN_EPS = 1e-05
        w1 = W1[language_ids]
        w2 = W2[language_ids]
        h = jnp.einsum('bsh,bha->bsa', hidden_states, w1) + b1[language_ids][:, None, :]
        h = jax.nn.relu(h)
        adapted = jnp.einsum('bsa,bah->bsh', h, w2) + b2[language_ids][:, None, :]
        x = hidden_states + adapted
        mean = jnp.mean(x, axis=-1, keepdims=True)
        var = jnp.mean(jnp.square(x - mean), axis=-1, keepdims=True)
        normed = (x - mean) * jax.lax.rsqrt(var + LN_EPS)
        return normed * gamma[language_ids][:, None, :] + beta[language_ids][:, None, :]

    def _L2_cond_ref(x, subject_id, weight, bias):
        import jax, jax.numpy as jnp
        import numpy as np
        S, O, H = (8, 256, 256)
        B, N = (32, 128)
        W = weight[subject_id]
        b = bias[subject_id]
        y = jnp.einsum('bnh,boh->bno', x, W) + b[:, None, :]
        return y

    def _L3_cond_ref(hidden, W1, b1, v, prompt_type_ids):
        import jax, jax.numpy as jnp
        import numpy as np
        NEG_INF = -1e+30
        B, S, D = hidden.shape
        attn_in = jnp.tanh(jnp.einsum('bsd,da->bsa', hidden, W1) + b1)
        scores = jnp.einsum('bsa,a->bs', attn_in, v)
        idx = jnp.arange(S)
        j = idx[:, None]
        l = idx[None, :]
        prefix_m = l <= j
        postfix_m = l >= j
        cloze_m = l != j
        pt = prompt_type_ids[:, None, None]
        mask = jnp.where(pt == 0, prefix_m[None], jnp.where(pt == 1, postfix_m[None], cloze_m[None]))
        masked_scores = jnp.where(mask, scores[:, None, :], NEG_INF)
        p = jax.nn.softmax(masked_scores, axis=-1)
        cnt = jnp.sum(mask, axis=-1).astype(hidden.dtype)
        pooled = jnp.einsum('bjl,bld->bjd', p, hidden) / cnt[..., None]
        return pooled
    x = x + _L0_cond_ref(x, fside_BxSxS_0, itok_B_18_1004, L0_cond_Wq, L0_cond_bq, L0_cond_Wk, L0_cond_bk, L0_cond_Wv, L0_cond_bv, L0_cond_Wo, L0_cond_bo, L0_cond_b_prev, L0_cond_b_self)
    x = x + _L1_cond_ref(x, itok_B_0_8, L1_cond_W1, L1_cond_b1, L1_cond_W2, L1_cond_b2, L1_cond_gamma, L1_cond_beta)
    x = x + _L2_cond_ref(x, itok_B_0_7, L2_cond_weight, L2_cond_bias)
    x = x + _L3_cond_ref(x, L3_cond_W1, L3_cond_b1, L3_cond_v, itok_B_0_2)
    return x

_drawn_inputs = setup_inputs


def setup_inputs(seed=0):
    import zlib

    import numpy as np

    out = dict(_drawn_inputs(seed))
    spreads = {'L0_cond_bq': (0.0, 0.8),
     'L0_cond_bk': (0.0, 2.0),
     'L0_cond_bv': (0.0, 1.009),
     'L0_cond_bo': (0.0, 0.28),
     'L1_cond_b1': (0.0, 0.8),
     'L1_cond_b2': (0.0, 0.8),
     'L1_cond_gamma': (1.0, 0.2),
     'L1_cond_beta': (0.0, 0.361)}
    factors = {'fside_BxSxS_0': 8.0,
     'L0_cond_Wq': 8.0,
     'L0_cond_Wk': 8.0,
     'L0_cond_Wv': 6.945,
     'L0_cond_b_prev': 8.0,
     'L0_cond_b_self': 8.0,
     'L2_cond_bias': 3.566,
     'L3_cond_W1': 4.089,
     'L3_cond_b1': 64.0,
     'L3_cond_v': 3.577}
    for name, (base, spread) in spreads.items():
        noise = np.random.default_rng([zlib.crc32(name.encode()), seed]).standard_normal(out[name].shape)
        drawn = base * np.exp(spread * noise) if base else spread * noise
        out[name] = jnp.asarray(drawn.astype(out[name].dtype))
    for name, factor in factors.items():
        out[name] = (out[name] * factor).astype(out[name].dtype)
    return out
```

```python
from contextlib import ExitStack

import numpy as np
import concourse.bass as bass
from concourse import mybir

F32 = mybir.dt.float32
F32R = mybir.dt.float32r
I32 = mybir.dt.int32
ALU = mybir.AluOpType
ACT = mybir.ActivationFunctionType
AX = mybir.AxisListType

B, S, D = 32, 256, 256
H, DH = 16, 16
P = 128
NC2 = D // P
PAIRS = H // 2
PH = PAIRS // 2
A1 = 64
LANG, SUBJ, KINDS = 10, 8, 3
VW = 32
NX = D + A1
NEG = -1e30
EPS = 1e-5
SCALE = 1.0 / 4.0
UNITS = 16
SPLIT = ((0, 0), (0, 1), (1, 0))
SK = 16 * (2 * 2 * 3 + PH)
FIRST, LAST = 4, 28
BANKS = 3

PIECES = [
    (0, "m1", 0), (2, "q", 2), (3, "num0", -1), (3, "x2T", -2), (4, "num1", -1), (5, "lin0", -2),
    (6, "lin1", -2), (6, "k", 2), (7, "aT", -1), (7, "ks", 2), (8, "v", 1), (9, "wo", -1),
    (10, "m0", 1), (10, "srep", -2), (11, "x1T", -1), (11, "ss", 2), (12, "pT", -2), (12, "vs", 1),
    (13, "h", -1), (14, "pool", -2), (15, "ad", -1),
]
NAMES = [n for _, n, _ in PIECES]
OFFSET = {n: o for _, n, o in PIECES}


def done(b, per=1, nth=None):
    nth = per if nth is None else nth
    if isinstance(b, int):
        return 0 if b < 0 else B * per if b >= B else b * per + nth
    return b * per + nth


def loaded(b, par):
    return max(0, 8 * (b - par) + 16) if isinstance(b, int) else 8 * (b - par) + 16


def before(b, unit):
    if isinstance(b, int):
        return max(0, min(b, B) * UNITS + unit) if b < B else B * UNITS
    return b * UNITS + unit


def block4(nc: bass.Bass, x, xT, sT, lens, lang, subj, kind, wq, bq, wk, bk, wv, bv, wo, bo, bprev,
           bself, w1, b1, w2, b2, gamma, beta, lw, lwT, lb, lbT, w3, b3, v3, ident_d, eye2_d,
           heads_d, kidx_d, pmask_d, out):
    ctx = ExitStack()
    with ctx:
        def sb(name, shape, dt=F32):
            return ctx.enter_context(nc.sbuf_tensor(name, shape, dt))

        def pb(name):
            return ctx.enter_context(nc.psum_tensor(name, [P, 512], F32))

        sems = {}

        def sem(name):
            if name not in sems:
                sems[name] = ctx.enter_context(nc.semaphore(name))
            return sems[name]

        qst = [sb(f"qst{i}", [P, PAIRS, 2 * S], F32R) for i in range(2)]
        kst = [sb(f"kst{i}", [P, PAIRS, S], F32R) for i in range(2)]
        xin = [sb(f"xin{i}", [P, NC2, S]) for i in range(2)]
        sin = [sb(f"sin{i}", [P, NC2, S]) for i in range(2)]
        xs = [[sb(f"xs{i}{r}", [P, NC2, S], F32R) for r in range(2)] for i in range(2)]
        ss = [[sb(f"ss{i}{r}", [P, NC2, S], F32R) for r in range(2)] for i in range(2)]
        qf = sb("qf", [P, 2, S])
        kf = sb("kf", [P, 2, S])
        pr = sb("pr", [P, 2, S])
        qp = [sb(f"qp{r}", [P, 2, S], F32R) for r in range(2)]
        kp = [sb(f"kp{r}", [P, 2, S], F32R) for r in range(2)]
        pp = [sb(f"pp{r}", [P, 2, S], F32R) for r in range(2)]
        nself = [sb(f"nself{i}", [P, 2, H]) for i in range(2)]
        mx = [sb(f"mx{i}", [P, 2, H]) for i in range(2)]
        mneg = [sb(f"mneg{i}", [P, 2, H], F32R) for i in range(2)]
        mrow = sb("mrow", [PAIRS, 2, P], F32R)
        earg = sb("earg", [P, 2, H])
        eself = [sb(f"eself{i}", [P, 2, H]) for i in range(2)]
        vaug = [sb(f"vaug{i}", [P, 2, H, VW]) for i in range(2)]
        vself = sb("vself", [P, 2, D])
        tv = [sb(f"tv{i}", [P, 2, D]) for i in range(2)]
        pt = sb("pt", [P, 2, 2, 4, S])
        pvt = sb("pvt", [P, 4, S])
        tot = sb("tot", [P, 2, H])
        rec = sb("rec", [P, 2, H])
        nv = sb("nv", [P, 2, D])
        att = nv
        aT = [sb(f"aT{r}", [P, NC2, S], F32R) for r in range(2)]
        xr = sb("xr", [P, 2, D])
        xb = xr
        x1 = sb("x1", [P, 2, D])
        x1b2 = sb("x1b2", [P, 2, D])
        x1be = sb("x1be", [P, 2, D])
        x1T = [sb(f"x1T{r}", [P, NC2, S], F32R) for r in range(2)]
        w1raw = sb("w1raw", [P, NC2, A1])
        w1p = [sb(f"w1p{r}", [P, NC2, 2, A1], F32R) for r in range(2)]
        w2raw = sb("w2raw", [P, D])
        w2p = [sb(f"w2p{r}", [P, D], F32R) for r in range(2)]
        b1c = sb("b1c", [P, 1])
        b2r = sb("b2r", [P, D])
        gar = sb("gar", [P, D])
        ber = sb("ber", [P, D])
        hst = sb("hst", [P, S], F32R)
        hf = sb("hf", [P, S])
        y = sb("y", [P, 2, D])
        st = sb("st", [P, 2, 6])
        mv = sb("mv", [P, 2, 2])
        veps = sb("veps", [P, 2])
        rstd = sb("rstd", [P, 2])
        mhalf = sb("mhalf", [P, 2])
        yn = sb("yn", [P, 2, D])
        yg = yn
        x2 = sb("x2", [P, 2, D])
        x2T = [sb(f"x2T{r}", [P, NC2, S], F32R) for r in range(2)]
        lwp = sb("lwp", [P, 2, NC2, NX], F32R)
        lbr = sb("lbr", [P, NX])
        x3 = sb("x3", [P, 2, NX])
        th = sb("th", [P, 2, A1])
        v3r = sb("v3r", [P, 2, A1])
        tvv = sb("tvv", [P, 2, A1])
        sc = sb("sc", [P, 2])
        pm = sb("pm", [P, 2, S + 1])
        msc = sb("msc", [P, 2, S])
        nm3 = sb("nm3", [P, 2])
        pe3 = sb("pe3", [P, 2, S])
        sum3 = sb("sum3", [P, 2])
        sc3 = sb("sc3", [P, 2])
        r3 = sb("r3", [P, 2])
        p3T = sb("p3T", [P, 2, S])
        ob = [sb(f"ob{i}", [P, 2, D]) for i in range(2)]
        W = {n: [sb(f"W{n}{r}", [P, NC2, D], F32R) for r in range(2)] for n in ("q", "k", "v", "o")}
        ident = sb("ident", [P, P])
        headsr = sb("headsr", [P, 2, H], F32R)
        heads = sb("heads", [P, 2, H])
        bqc = sb("bqc", [P, 2])
        bkc = sb("bkc", [P, 2])
        bsc = sb("bsc", [P, 2])
        bop = sb("bop", [P, D])
        idx = sb("idx", [1, 3, B], I32)
        flat = pt[:, :, :, :, :].rearrange("p a b c d -> p (a b c d)")
        raw = {n: flat[:, 512 * i:512 * i + 512].rearrange("p (c n) -> p c n", c=NC2)
               for i, n in enumerate(("q", "k", "v", "o"))}
        lwn = [flat[:, 2048 + 512 * i:2560 + 512 * i].rearrange("p (c n) -> p c n", c=NC2) for i in range(2)]
        lcat = [flat[:, 3072 + 320 * 2 * i:3072 + 320 * 2 * (i + 1)].rearrange("p (c n) -> p c n", c=NC2)
                for i in range(1)] + [x3[:, :, :]]
        eye2 = y
        w3s = x1b2[:, 0, 0:2 * A1].rearrange("p (c n) -> p c n", c=NC2)
        bvb = x1[:, :, 0:P]
        bcol = msc[:, 0, 0:16]
        lbTs = msc[:, 1, 0:16].rearrange("p (c s) -> p c s", c=NC2)
        btab = tv[0][0:SUBJ, :, :].rearrange("p a b -> p (a b)")[:, 0:NX]
        b3s = att[0:SUBJ, 1, 0:A1]
        bos = x1be[:, 0, :]
        kid = yn[0:B, 0, :]
        mrows = hst[0:B, :]
        lenf = sb("lenf", [B, 1])
        leni = sb("leni", [B, 1], I32)

        SN = [pb(f"SN{i}") for i in range(2)]
        ST = [pb(f"ST{i}") for i in range(2)]
        PV = pb("PV")
        M = [pb(f"M{i}") for i in range(BANKS)]
        bank = {n: M[i % BANKS] for i, n in enumerate(NAMES)}

        lws_d = nc.dram_tensor("lws", [SUBJ, P, 2 * NC2 * NX], F32, kind="Internal").ap()
        lbs_d = nc.dram_tensor("lbs", [SUBJ, NX], F32, kind="Internal").ap()
        mrow_d = nc.dram_tensor("mrows", [B, S], F32, kind="Internal").ap()

        lwst = [lwp[:, :, :, :], kst[1][:, :, :].rearrange("p a n -> p (a n)")[:, 0:2 * NC2 * NX].rearrange(
            "p (r c n) -> p r c n", r=2, c=NC2)]
        xT3, sT3 = (a.rearrange("b (c p) n -> b p c n", p=P) for a in (xT, sT))
        x4, o4 = (a.rearrange("b (c p) n -> b p c n", p=P) for a in (x, out))
        w1v = w1.rearrange("l (c p) n -> l p c n", p=P)
        pm3 = pmask_d.rearrange("k (c p) n -> k p c n", p=P)

        ld_w = sem("ld_w")
        ld_l = [sem("ld_l0"), sem("ld_l1")]
        set_dve = sem("set_dve")
        set_pe = sem("set_pe")
        set_act = sem("set_act")
        fold = sem("fold")
        cat = sem("cat")
        eyed = sem("eyed")
        lsplit = sem("lsplit")
        lsaved = sem("lsaved")
        saved = sem("saved")
        ready = sem("ready")

        block = ctx.enter_context(nc.Block())
        WL = 19

        def at_work(t):
            if not isinstance(t, int):
                return dict.fromkeys("ABCEF", True)
            return {n: 0 <= t + o < B for n, o in zip("ABCEF", (2, 1, 0, -1, -2))}

        def steps(eng, step):
            for t in range(-2, FIRST):
                step(t, t % 2)
            with eng.Fori(FIRST, LAST, 2) as t:
                step(t, 0)
                step(t + 1, 1)
            for t in range(LAST, B + 2):
                step(t, t % 2)

        def tokens(a):
            return a.rearrange("(c p) n -> p c n", p=P)

        @block.sync
        def _(sp):
            loads = [(raw["q"], tokens(wq)), (raw["k"], tokens(wk)), (raw["v"], tokens(wv)),
                     (raw["o"], tokens(wo)), (ident[:], ident_d), (eye2[:], tokens(eye2_d)),
                     (heads[:], heads_d), (bcol[:, 0:2], bq), (bcol[:, 2:4], bk), (bcol[:, 4:6], bself),
                     (bcol[:, 6:8], bprev), (bcol[:, 8:10], bv), (bos, bo.to_broadcast([P, D])),
                     (w3s, tokens(w3)), (lbTs, tokens(lbT)), (kid, kidx_d), (leni[:], lens),
                     (btab[:, 0:D], lb), (b3s, b3.to_broadcast([SUBJ, A1]))]
            assert len(loads) == WL
            with nc.allow_non_contiguous_dma(reason="small constants"):
                for dst, src in loads:
                    sp.dma_start(dst, src).then_inc(ld_w, 16)
            sp.dma_start(idx[:, 0, :], lang).then_inc(sem("ld_i"), 16)
            sp.dma_start(idx[:, 1, :], subj).then_inc(sem("ld_i"), 16)
            sp.dma_start(idx[:, 2, :], kind).then_inc(sem("ld_i"), 16)
            for i in range(2):
                sp.dma_start(v3r[:, i, :], v3.to_broadcast([P, A1])).then_inc(sem("ld_v3"), 16)
            sp.wait_ge(sem("mask_split"), 1)
            sp.dma_start(mrow_d, mrows.bitcast(F32)).then_inc(saved, 16)
            sp.wait_ge(sem("btab"), 1)
            sp.dma_start(lbs_d, btab).then_inc(saved, 16)
            for i in range(2):
                sp.dma_start(lcat[i][:, :, 0:D], tokens(lwT[i])).then_inc(ld_l[i], 16)
                sp.dma_start(lwn[i], tokens(lw[i])).then_inc(ld_l[i], 16)
            for j in range(SUBJ):
                i = j % 2
                sp.wait_ge(lsplit, j + 1)
                sp.dma_start(lws_d[j], lwst[i].rearrange("p a b n -> p (a b n)").bitcast(F32)).then_inc(lsaved, 16)
                if j + 2 < SUBJ:
                    sp.wait_ge(fold, j + 1)
                    sp.dma_start(lcat[i][:, :, 0:D], tokens(lwT[j + 2])).then_inc(ld_l[i], 16)
                    sp.dma_start(lwn[i], tokens(lw[j + 2])).then_inc(ld_l[i], 16)
            sp.wait_ge(saved, 32)
            sp.wait_ge(lsaved, 16 * SUBJ)
            sp.wait_ge(sem("ld_i"), 48)

            def which(k, b, most):
                return sp.value_load(idx[0:1, k, bass.ds(b, 1)], min_val=0, max_val=most)

            def stacks(half, b, par):
                at, pairs = slice(64 * half, 64 * half + 64), slice(PH * half, PH * half + PH)
                sm = sem(f"stack{half}")
                for e in range(2):
                    for r in range(3):
                        row = 48 * e + 16 * r
                        sp.dma_start(qst[par][row:row + 16, pairs, e * S:e * S + S].bitcast(F32),
                                     qp[r % 2][at, e, :].bitcast(F32)).then_inc(sm, 16)
                        sp.dma_start(kst[par][row:row + 16, pairs, :].bitcast(F32),
                                     kp[r // 2][at, e, :].bitcast(F32)).then_inc(sm, 16)
                for p in range(PH * half, PH * half + PH):
                    sp.dma_start(kst[par][96:97, p, :].bitcast(F32), mrow_d[bass.ds(b, 1), :]).then_inc(sm, 16)

            def step(t, par):
                on = at_work(t)
                odd = 1 - par
                if on["B"]:
                    sp.wait_ge(saved, 32)
                    sp.wait_ge(sem("ksplit"), done(t + 1))
                    sp.wait_ge(sem("qsplit"), done(t + 1))
                    sp.wait_ge(sem("st_ready"), done(t - 1, UNITS))
                    stacks(1, t + 1, odd)
                if on["C"]:
                    sp.wait_ge(saved, 32)
                    sp.wait_ge(sem("mrow1"), done(t))
                    sp.dma_start(qst[par][97:98, PH:PAIRS, :].bitcast(F32), mrow[:, :, :].bitcast(F32)).then_inc(sem("mput1"), 16)
                if not isinstance(t, int) or 0 <= t + 3 < B or t == -2:
                    for b, i in ([(0, 0), (1, 1)] if isinstance(t, int) and t == -2 else [(t + 3, odd)]):
                        sp.wait_ge(saved, 32)
                        sp.wait_ge(sem("xsplit"), done(b - 2))
                        sp.wait_ge(sem("ssplit"), done(b - 2))
                        sp.dma_start(xin[i][:], xT3[b]).then_inc(sem(f"ld_x{i}"), 16)
                        sp.dma_start(sin[i][:], sT3[b]).then_inc(sem(f"ld_s{i}"), 16)
                if on["E"]:
                    la = which(0, t - 1, LANG - 1)
                    sp.wait_ge(saved, 32)
                    sp.wait_ge(sem("gained"), done(t - 2))
                    sp.dma_start(gar[:], gamma[bass.ds(la, 1), :].to_broadcast([P, D])).then_inc(sem("ld_ga"), 16)
                if on["E"]:
                    su = which(1, t - 1, SUBJ - 1)
                    ki = which(2, t - 1, KINDS - 1)
                    sp.wait_ge(saved, 32)
                    sp.wait_ge(sem("lin"), done(t - 2, 2))
                    sp.dma_start(lwp[:].rearrange("p a b n -> p (a b n)").bitcast(F32), lws_d[su]).then_inc(sem("ld_lw"), 16)
                    sp.wait_ge(saved, 32)
                    sp.wait_ge(sem("x3"), done(t - 2, 2))
                    sp.dma_start(lbr[:], lbs_d[bass.ds(su, 1), :].to_broadcast([P, NX])).then_inc(sem("ld_lb"), 16)
                if on["A"]:
                    sp.wait_ge(saved, 32)
                    sp.wait_ge(sem("ksplit"), done(t + 2))
                    sp.wait_ge(sem("qsplit"), done(t + 2))
                    sp.wait_ge(sem("st_ready"), done(t, UNITS, UNITS // 2))
                    stacks(0, t + 2, par)
                if on["C"]:
                    la = which(0, t, LANG - 1)
                    sp.wait_ge(saved, 32)
                    sp.wait_ge(sem("wsplit"), done(t - 1))
                    sp.dma_start(w1raw[:], w1v[la]).then_inc(sem("ld_w12"), 16)
                    for i in range(2):
                        sp.dma_start(w2raw[64 * i:64 * i + 64, :], w2[la]).then_inc(sem("ld_w12"), 16)
                if on["B"]:
                    sp.wait_ge(saved, 32)
                    sp.wait_ge(sem("mrow0"), done(t + 1))
                    sp.dma_start(qst[odd][97:98, 0:PH, :].bitcast(F32), mrow[:, :, :].bitcast(F32)).then_inc(sem("mput0"), 16)
                if on["C"]:
                    sp.wait_ge(saved, 32)
                    sp.wait_ge(sem("x1"), done(t - 1))
                    sp.dma_start(xr[:], x4[t]).then_inc(sem("ld_xr"), 16)
                    sp.wait_ge(saved, 32)
                    sp.wait_ge(sem("x1sum"), done(t - 1))
                    sp.dma_start(b2r[:], b2[bass.ds(la, 1), :].to_broadcast([P, D])).then_inc(sem("ld_b"), 16)
                    sp.dma_start(ber[:], beta[bass.ds(la, 1), :].to_broadcast([P, D])).then_inc(sem("ld_b"), 16)
                    sp.wait_ge(saved, 32)
                    sp.wait_ge(sem("hlo"), done(t - 1))
                    with nc.allow_non_contiguous_dma(reason="a bias a partition"):
                        for i in range(2):
                            sp.dma_start(b1c[64 * i:64 * i + 64, :], b1[la]).then_inc(sem("ld_b1"), 16)
                if on["E"]:
                    sp.wait_ge(saved, 32)
                    sp.wait_ge(sem("masked"), done(t - 2))
                    sp.wait_ge(sem("r3"), done(t - 2))
                    sp.dma_start(pm[:], pm3[ki]).then_inc(sem("ld_pm"), 16)
                if on["F"]:
                    sp.wait_ge(saved, 32)
                    sp.wait_ge(sem("outs"), done(t - 2, 2))
                    sp.dma_start(o4[t - 2], ob[par][:]).then_inc(sem(f"stored{par}"), 16)

            steps(sp, step)
            for i in range(2):
                sp.wait_ge(sem(f"stored{i}"), 16 * B // 2)


        @block.tensor
        def _(pe):
            def three(dst, left, right):
                n = 0
                for c in range(NC2):
                    for a, b in SPLIT:
                        last = nc.tensor.matmul(dst, left(a, c), right(b, c), start=n == 0, stop=n == 5)
                        n += 1
                return last

            def turn(dst, src):
                for c in range(NC2):
                    for i in range(2):
                        last = nc.tensor.transpose(dst[:, c * S + i * P:c * S + i * P + P],
                                                   src[:, i, c * P:c * P + P], ident[:])
                return last

            pe.wait_ge(ld_w, 16 * WL)
            for n, w, col in ((0, "q", 4), (2, "k", 6), (4, "k", 4)):
                for e in range(2):
                    for c in range(NC2):
                        nc.tensor.matmul(M[0][:, n + e:n + e + 1], raw[w][:, c, e * P:e * P + P],
                                         bcol[:, col + c:col + c + 1], start=c == 0, stop=c == 1)
            pe.wait_ge(set_dve, 2)
            for c in range(NC2):
                nc.tensor.matmul(M[1][:, 0:D], bvb[:, c, :], raw["o"][:, c, :], start=c == 0, stop=c == 1)
            for c in range(NC2):
                last = nc.tensor.matmul(M[2][0:SUBJ, 0:A1], lbTs[:, c, 0:SUBJ], w3s[:, c, :],
                                        start=c == 0, stop=c == 1)
            last.then_inc(set_pe, 1)
            for j in range(SUBJ):
                i = j % 2
                pe.wait_ge(eyed, j + 1)
                if j >= 2:
                    pe.wait_ge(lsplit, j - 1)
                for hc in range(NC2):
                    for oc in range(NC2):
                        last = nc.tensor.matmul(SN[i][:, hc * A1:hc * A1 + A1], lwn[i][:, oc, hc * P:hc * P + P],
                                                w3s[:, oc, :], start=oc == 0, stop=oc == 1)
                last.then_inc(fold, 1)
            pe.wait_ge(ready, 1)

            READER = {"q": ("qf", 1, 1), "k": ("kf", 1, 1), "ks": ("prod", 1, 1), "v": ("v", 1, 1),
                      "vs": ("vself", 1, 1), "ss": ("nself", 1, 1), "m0": ("mrow0", 1, 1),
                      "m1": ("mrow1", 1, 1), "num0": ("nv", 2, 1), "num1": ("nv", 2, 2),
                      "aT": ("aTlo", 1, 1), "wo": ("x1", 1, 1), "x1T": ("x1Tlo", 1, 1), "h": ("hlo", 1, 1),
                      "ad": ("y", 1, 1), "x2T": ("x2Tlo", 1, 1), "lin0": ("x3", 2, 1), "lin1": ("x3", 2, 2),
                      "srep": ("masked", 1, 1), "pT": ("p3T", 1, 1), "pool": ("outs", 2, 2)}

            def step(t, par):
                on = at_work(t)
                odd = 1 - par

                def runs(name, u):
                    return not isinstance(u, int) or 0 <= u + OFFSET[name] < B

                def free(name):
                    k, u = NAMES.index(name), t
                    while True:
                        k -= BANKS
                        if k < 0:
                            k, u = (len(NAMES) - 1) - (len(NAMES) - 1 - (k + BANKS)) % BANKS, u - 1
                        if isinstance(u, int) and u < -2:
                            return
                        if runs(NAMES[k], u):
                            s, per, nth = READER[NAMES[k]]
                            pe.wait_ge(sem(s), done(u + OFFSET[NAMES[k]], per, nth))
                            return

                def group(g, b, i):
                    pe.wait_ge(sem("exp_done"), before(b, 4 * g + 4))
                    pe.wait_ge(sem("v"), done(b))
                    if g % 2 == 0:
                        pe.wait_ge(sem("pvt"), done(b - 1, 2) if g == 0 else done(b, 2, 1))
                    for kb in range(2):
                        for j in range(4):
                            last = nc.tensor.matmul(PV[32 * j:32 * j + 32, (g % 2) * S:(g % 2) * S + S],
                                                    vaug[i][:, kb, 4 * g + j, :], pt[:, g % 2, kb, j, :],
                                                    start=kb == 0, stop=kb == 1)
                    last.then_inc(sem("pv_done"), 1)

                for s in range(UNITS):
                    if on["C"]:
                        if s == 0 or s == UNITS // 2:
                            pe.wait_ge(sem(f"mput{s // 8}"), done(t, 16))
                        pe.wait_ge(sem("exp_done"), before(t, s - 1) if s else before(t - 1, UNITS - 1))
                        pair, kb = s // 2, s % 2
                        nc.tensor.matmul(ST[s % 2][:], kst[par][0:98, pair, kb * P:kb * P + P],
                                         qst[par][0:98, pair, :], start=True, stop=True).then_inc(sem("st_ready"), 1)
                    if on["B"]:
                        if s == 0 or s == UNITS // 2:
                            pe.wait_ge(sem(f"stack{s // 8}"), done(t + 1, SK))
                        pe.wait_ge(sem("maxed"), before(t + 1, s - 1) if s else before(t, UNITS - 1))
                        pair, qb = s // 2, s % 2
                        for e in range(2):
                            last = nc.tensor.matmul(SN[s % 2][:, e * S:e * S + S],
                                                    qst[odd][0:97, pair, e * S + qb * P:e * S + qb * P + P],
                                                    kst[odd][0:97, pair, :], start=True, stop=True)
                        last.then_inc(sem("sn_ready"), 1)
                    for half, slot, b, i in ((1, 0, t, par), (0, 10, t + 1, odd)):
                        if s == slot and on["BC"[half]]:
                            free(f"m{half}")
                            pe.wait_ge(sem(f"mneg{half}"), done(b))
                            for c in range(2):
                                last = nc.tensor.transpose(bank[f"m{half}"][0:8, c * P:c * P + P],
                                                           mneg[i][:, c, 8 * half:8 * half + 8].bitcast(F32), ident[:])
                            last.then_inc(sem(f"m{half}_pe"), 1)
                    if s == 1 and on["E"]:
                        group(3, t - 1, odd)
                    if s == 2 and on["A"]:
                        free("q")
                        pe.wait_ge(sem("shi"), done(t + 2))
                        pe.wait_ge(sem("ssplit"), done(t + 2))
                        for e in range(2):
                            last = three(bank["q"][:, e * S:e * S + S], lambda r, c: W["q"][r][:, c, e * P:e * P + P],
                                         lambda r, c: ss[par][r][:, c, :])
                        last.then_inc(sem("q_pe"), 1)
                    for i, slot in ((0, 3), (1, 4)):
                        if s == slot and on["E"]:
                            free(f"num{i}")
                            pe.wait_ge(sem("pvt"), done(t - 1, 2))
                            for g in range(4):
                                last = nc.tensor.transpose(bank[f"num{i}"][:, g * P:g * P + P],
                                                           pvt[:, g, i * P:i * P + P], ident[:])
                            last.then_inc(sem("num_pe"), 1)
                    if s == 3 and on["F"]:
                        free("x2T")
                        pe.wait_ge(sem("x2"), done(t - 2))
                        turn(bank["x2T"], x2).then_inc(sem("x2T_pe"), 1)
                    for i in range(2):
                        if s == 5 + i and on["F"]:
                            free(f"lin{i}")
                            pe.wait_ge(sem("x2Thi"), done(t - 2))
                            pe.wait_ge(sem("x2Tlo"), done(t - 2))
                            pe.wait_ge(sem("ld_lw"), done(t - 2, 16))
                            three(bank[f"lin{i}"][:, 0:NX], lambda r, c: x2T[r][:, c, i * P:i * P + P],
                                  lambda r, c: lwp[:, r, c, :]).then_inc(sem("lin"), 1)
                    if s in (5, 9, 13) and on["C"]:
                        group(s // 4 - 1, t, par)
                    if s == 6 and on["A"]:
                        free("k")
                        pe.wait_ge(sem("xhi"), done(t + 2))
                        pe.wait_ge(sem("xsplit"), done(t + 2))
                        for e in range(2):
                            last = three(bank["k"][:, e * S:e * S + S], lambda r, c: W["k"][r][:, c, e * P:e * P + P],
                                         lambda r, c: xs[par][r][:, c, :])
                        last.then_inc(sem("k_pe"), 1)
                    if s == 7 and on["E"]:
                        free("aT")
                        pe.wait_ge(sem("att"), done(t - 1))
                        turn(bank["aT"], att).then_inc(sem("aT_pe"), 1)
                    if s == 7 and on["A"]:
                        free("ks")
                        for e in range(2):
                            last = three(bank["ks"][:, e * S:e * S + S], lambda r, c: W["k"][r][:, c, e * P:e * P + P],
                                         lambda r, c: ss[par][r][:, c, :])
                        last.then_inc(sem("ks_pe"), 1)
                    for name, slot, src, w, b in (("v", 8, xs[odd], W["v"], "B"), ("vs", 12, ss[odd], W["v"], "B")):
                        if s == slot and on[b]:
                            free(name)
                            for i in range(2):
                                last = three(bank[name][:, i * D:i * D + D], lambda r, c: src[r][:, c, i * P:i * P + P],
                                             lambda r, c: w[r][:, c, :])
                            last.then_inc(sem(f"{name}_pe"), 1)
                    if s == 9 and on["E"]:
                        free("wo")
                        pe.wait_ge(sem("aThi"), done(t - 1))
                        pe.wait_ge(sem("aTlo"), done(t - 1))
                        for i in range(2):
                            last = three(bank["wo"][:, i * D:i * D + D], lambda r, c: aT[r][:, c, i * P:i * P + P],
                                         lambda r, c: W["o"][r][:, c, :])
                        last.then_inc(sem("wo_pe"), 1)
                    if s == 10 and on["F"]:
                        free("srep")
                        pe.wait_ge(sem("sc"), done(t - 2))
                        for i in range(2):
                            last = nc.tensor.transpose(bank["srep"][:, i * P:i * P + P],
                                                       sc[:, i:i + 1].to_broadcast([P, P]), ident[:])
                        last.then_inc(sem("srep_pe"), 1)
                    if s == 11 and on["E"]:
                        free("x1T")
                        pe.wait_ge(sem("x1"), done(t - 1))
                        turn(bank["x1T"], x1).then_inc(sem("x1T_pe"), 1)
                    if s == 11 and on["A"]:
                        free("ss")
                        pe.wait_ge(sem("phi"), done(t + 2))
                        pe.wait_ge(sem("psplit"), done(t + 2))
                        for i in range(2):
                            n = 0
                            for e in range(2):
                                for r in range(2):
                                    last = nc.tensor.matmul(bank["ss"][:, i * H:i * H + H],
                                                            pp[r][:, e, i * P:i * P + P], headsr[:, e, :],
                                                            start=n == 0, stop=n == 3)
                                    n += 1
                        last.then_inc(sem("ss_pe"), 1)
                    if s == 12 and on["F"]:
                        free("pT")
                        pe.wait_ge(sem("pe3"), done(t - 2, 2))
                        turn(bank["pT"], pe3).then_inc(sem("pT_pe"), 1)
                    if s == 13 and on["E"]:
                        free("h")
                        pe.wait_ge(sem("x1Thi"), done(t - 1))
                        pe.wait_ge(sem("x1Tlo"), done(t - 1))
                        pe.wait_ge(sem("wlo"), done(t - 1))
                        pe.wait_ge(sem("wsplit"), done(t - 1))
                        three(bank["h"][:, 0:S], lambda r, c: w1p[r][:, c, :, :].rearrange("p a n -> p (a n)"),
                              lambda r, c: x1T[r][:, c, :]).then_inc(sem("h_pe"), 1)
                    if s == 14 and on["F"]:
                        free("pool")
                        pe.wait_ge(sem("p3T"), done(t - 2))
                        for i in range(2):
                            for c in range(2):
                                last = nc.tensor.matmul(bank["pool"][:, i * D:i * D + D], p3T[:, c, i * P:i * P + P],
                                                        x3[:, c, 0:D], start=c == 0, stop=c == 1)
                        last.then_inc(sem("pool_pe"), 1)
                    if s == 15 and on["E"]:
                        free("ad")
                        pe.wait_ge(sem("hhi"), done(t - 1))
                        pe.wait_ge(sem("hlo"), done(t - 1))
                        for i in range(2):
                            for r in range(2):
                                last = nc.tensor.matmul(bank["ad"][:, i * D:i * D + D], hst[:, i * P:i * P + P],
                                                        w2p[r][:], start=r == 0, stop=r == 1)
                        last.then_inc(sem("ad_pe"), 1)

            steps(pe, step)

        @block.gpsimd
        def _(pool):
            nc.gpsimd.memset(mhalf[:], -0.5).then_inc(sem("pool_set"), 1)
            pool.wait_ge(sem("pool_set"), 1)
            pool.wait_ge(ready, 1)

            def hi(dst, src):
                pool.sem_inc(sem("waited_pool"), 1)
                return nc.gpsimd.tensor_scalar(dst, src, 1.0, 0.0, ALU.mult, ALU.add)

            def lo(dst, src, high):
                return nc.gpsimd.tensor_tensor(dst, src, high.bitcast(F32), ALU.subtract)

            def step(t, par):
                on = at_work(t)
                odd = 1 - par
                if on["A"]:
                    pool.wait_ge(sem("shi"), done(t + 2))
                    pool.wait_ge(sem("vs_pe"), done(t))
                    lo(ss[par][1][:], sin[par][:], ss[par][0][:]).then_inc(sem("ssplit"), 1)
                    pool.wait_ge(sem("xhi"), done(t + 2))
                    pool.wait_ge(sem("v_pe"), done(t))
                    lo(xs[par][1][:], xin[par][:], xs[par][0][:]).then_inc(sem("xsplit"), 1)
                if on["F"]:
                    pool.wait_ge(sem("var"), done(t - 2))
                    pool.wait_ge(sem("normed"), done(t - 3))
                    pool.sem_inc(sem("waited_pool"), 1)
                    nc.gpsimd.tensor_scalar(veps[:], mv[:, :, 1], 1.0, EPS, ALU.mult, ALU.add).then_inc(sem("veps"), 1)
                    pool.wait_ge(sem("veps"), done(t - 2))
                    nc.gpsimd.tensor_tensor(rstd[:], veps[:], mhalf[:], ALU.pow).then_inc(sem("rstd"), 1)
                    pool.wait_ge(sem("normed"), done(t - 2))
                    pool.wait_ge(sem("ld_ga"), done(t - 2, 16))
                    nc.gpsimd.tensor_tensor(yg[:], yn[:], gar[:].unsqueeze(1).to_broadcast([P, 2, D]),
                                            ALU.mult).then_inc(sem("gained"), 1)
                if on["C"]:
                    pool.wait_ge(sem("eself"), done(t))
                    pool.wait_ge(sem("vself"), done(t))
                    pool.wait_ge(sem("nv"), done(t - 2, 2))
                    nc.gpsimd.tensor_tensor(tv[par][:].rearrange("p c (h d) -> p c h d", d=DH),
                                            vself[:].rearrange("p c (h d) -> p c h d", d=DH),
                                            eself[par][:].unsqueeze(3).to_broadcast([P, 2, H, DH]),
                                            ALU.mult).then_inc(sem("tv"), 1)
                if on["A"]:
                    pool.wait_ge(sem("qf"), done(t + 2))
                    pool.wait_ge(sem("stack0"), done(t + 1, SK))
                    pool.wait_ge(sem("stack1"), done(t + 1, SK))
                    hi(qp[0][:], qf[:]).then_inc(sem("qhi"), 1)
                    pool.wait_ge(sem("qhi"), done(t + 2))
                    lo(qp[1][:], qf[:], qp[0][:]).then_inc(sem("qsplit"), 1)
                if on["E"]:
                    pool.wait_ge(sem("nv"), done(t - 1, 2))
                    pool.wait_ge(sem("rec"), done(t - 1, 2))
                    nc.gpsimd.tensor_tensor(att[:].rearrange("p c (h d) -> p c h d", d=DH),
                                            nv[:].rearrange("p c (h d) -> p c h d", d=DH),
                                            rec[:].unsqueeze(3).to_broadcast([P, 2, H, DH]),
                                            ALU.mult).then_inc(sem("att"), 1)
                if on["A"]:
                    pool.wait_ge(sem("kf"), done(t + 2))
                    hi(kp[0][:], kf[:]).then_inc(sem("khi"), 1)
                    pool.wait_ge(sem("khi"), done(t + 2))
                    lo(kp[1][:], kf[:], kp[0][:]).then_inc(sem("ksplit"), 1)
                if on["E"]:
                    pool.wait_ge(sem("ld_xr"), done(t - 1, 16))
                    nc.gpsimd.tensor_tensor(xb[:], xr[:], bop[:].unsqueeze(1).to_broadcast([P, 2, D]),
                                            ALU.add).then_inc(sem("xb"), 1)
                if on["A"]:
                    pool.wait_ge(sem("prod"), done(t + 2))
                    pool.wait_ge(sem("ss_pe"), done(t + 1))
                    hi(pp[0][:], pr[:]).then_inc(sem("phi"), 1)
                    pool.wait_ge(sem("phi"), done(t + 2))
                    lo(pp[1][:], pr[:], pp[0][:]).then_inc(sem("psplit"), 1)
                if on["E"]:
                    pool.wait_ge(sem("ld_w12"), done(t - 1, 48))
                    pool.wait_ge(sem("h_pe"), done(t - 2))
                    pool.wait_ge(sem("ad_pe"), done(t - 2))
                    twice = w1raw[:].unsqueeze(2).to_broadcast([P, NC2, 2, A1])
                    hi(w1p[0][:], twice).then_inc(sem("whi"), 1)
                    hi(w2p[0][:], w2raw[:]).then_inc(sem("whi"), 1)
                    pool.wait_ge(sem("whi"), done(t - 1, 2))
                    lo(w1p[1][:], twice, w1p[0][:]).then_inc(sem("wlo"), 1)
                    lo(w2p[1][:], w2raw[:], w2p[0][:]).then_inc(sem("wsplit"), 1)
                    pool.wait_ge(sem("x1"), done(t - 1))
                    pool.wait_ge(sem("ld_b"), done(t - 1, 32))
                    pool.wait_ge(sem("y"), done(t - 2))
                    nc.gpsimd.tensor_tensor(x1b2[:], x1[:], b2r[:].unsqueeze(1).to_broadcast([P, 2, D]),
                                            ALU.add).then_inc(sem("x1b2"), 1)
                    pool.wait_ge(sem("x2"), done(t - 2))
                    nc.gpsimd.tensor_tensor(x1be[:], x1[:], ber[:].unsqueeze(1).to_broadcast([P, 2, D]),
                                            ALU.add).then_inc(sem("x1sum"), 1)

            steps(pool, step)

        @block.scalar
        def _(act):
            def copy(dst, src, bias=0.0):
                return nc.scalar.activation(dst, src, ACT.Identity, bias=bias)

            act.wait_ge(ready, 1)

            def step(t, par):
                on = at_work(t)
                odd = 1 - par
                for s in range(UNITS):
                    g, kb = s // 4, s % 2
                    if on["C"]:
                        act.wait_ge(sem("st_ready"), before(t, s + 1))
                        if s % 4 == 0:
                            act.wait_ge(sem("pv_done"), max(0, 4 * t + g - 1) if isinstance(t, int) else 4 * t + g - 1)
                        nc.scalar.activation(pt[:, g % 2, kb, 2 * (s // 2 % 2):2 * (s // 2 % 2) + 2, :],
                                             ST[s % 2][:].rearrange("p (h q) -> p h q", h=2), ACT.Exp,
                                             scale=SCALE).then_inc(sem("exp_done"), 1)
                    if s == 0 and on["C"]:
                        act.wait_ge(sem("m1_pe"), done(t))
                        act.wait_ge(sem("mput0"), done(t, 16))
                        copy(mrow[:], bank["m1"][0:PAIRS, 0:S].rearrange("p (c q) -> p c q", c=2)).then_inc(sem("mrow1"), 1)
                        act.wait_ge(sem("earg"), done(t))
                        act.wait_ge(sem("tv"), done(t - 2))
                        act.wait_ge(sem("tot"), done(t - 2, 2))
                        nc.scalar.activation(eself[par][:], earg[:], ACT.Exp, scale=SCALE).then_inc(sem("eself"), 1)
                    if s == 0 and on["A"]:
                        act.wait_ge(sem(f"ld_s{par}"), loaded(t + 2, par))
                        act.wait_ge(sem("vs_pe"), done(t))
                        copy(ss[par][0][:], sin[par][:]).then_inc(sem("shi"), 1)
                    if s == 1 and on["A"]:
                        act.wait_ge(sem(f"ld_x{par}"), loaded(t + 2, par))
                        act.wait_ge(sem("v_pe"), done(t))
                        copy(xs[par][0][:], xin[par][:]).then_inc(sem("xhi"), 1)
                    if s == 2 and on["E"]:
                        act.wait_ge(sem("pv_done"), done(t - 1, 4))
                        act.wait_ge(sem("num_pe"), done(t - 2, 2))
                        copy(pvt[:, 2:4, :], PV[:].rearrange("p (g q) -> p g q", g=2)).then_inc(sem("pvt"), 1)
                    if s == 3 and on["A"]:
                        act.wait_ge(sem("q_pe"), done(t + 2))
                        act.wait_ge(sem("qsplit"), done(t + 1))
                        act.wait_ge(sem("prod"), done(t + 1))
                        for e in range(2):
                            copy(qf[:, e, :], bank["q"][:, e * S:e * S + S], bqc[:, e:e + 1]).then_inc(sem("qe" if e == 0 else "qf"), 1)
                    if s == 4 and on["F"]:
                        act.wait_ge(sem("x2T_pe"), done(t - 2))
                        act.wait_ge(sem("lin"), done(t - 3, 2))
                        copy(x2T[0][:], bank["x2T"][:].rearrange("p (c q) -> p c q", c=2)).then_inc(sem("x2Thi"), 1)
                    if s == 7 and on["A"]:
                        act.wait_ge(sem("k_pe"), done(t + 2))
                        act.wait_ge(sem("ksplit"), done(t + 1))
                        for e in range(2):
                            copy(kf[:, e, :], bank["k"][:, e * S:e * S + S], bkc[:, e:e + 1]).then_inc(sem("ke" if e == 0 else "kf"), 1)
                    if s == 7 and on["F"]:
                        act.wait_ge(sem("x3"), done(t - 2, 2))
                        act.wait_ge(sem("tvv"), done(t - 3))
                        nc.scalar.activation(th[:], x3[:, :, D:NX], ACT.Tanh).then_inc(sem("tanh"), 1)
                    if s == 8 and on["E"]:
                        act.wait_ge(sem("aT_pe"), done(t - 1))
                        act.wait_ge(sem("wo_pe"), done(t - 2))
                        copy(aT[0][:], bank["aT"][:].rearrange("p (c q) -> p c q", c=2)).then_inc(sem("aThi"), 1)
                    if s == 9 and on["B"]:
                        act.wait_ge(sem("v_pe"), done(t + 1))
                        act.wait_ge(sem("pv_done"), done(t - 1, 4))
                        copy(vaug[odd][:, :, :, 0:DH],
                             bank["v"][:].rearrange("p (c h d) -> p c h d", c=2, d=DH)).then_inc(sem("v"), 1)
                    if s == 10 and on["C"]:
                        act.wait_ge(sem("pv_done"), done(t, 4, 2))
                        act.wait_ge(sem("num_pe"), done(t - 1, 2))
                        copy(pvt[:, 0:2, :], PV[:].rearrange("p (g q) -> p g q", g=2)).then_inc(sem("pvt"), 1)
                    if s == 10 and on["B"]:
                        act.wait_ge(sem("m0_pe"), done(t + 1))
                        act.wait_ge(sem("mput1"), done(t, 16))
                        copy(mrow[:], bank["m0"][0:PAIRS, 0:S].rearrange("p (c q) -> p c q", c=2)).then_inc(sem("mrow0"), 1)
                    if s == 11 and on["F"]:
                        act.wait_ge(sem("nm3"), done(t - 2))
                        act.wait_ge(sem("pT_pe"), done(t - 3))
                        act.wait_ge(sem("r3"), done(t - 3))
                        for i in range(2):
                            nc.scalar.activation(pe3[:, i, :], msc[:, i, :], ACT.Exp, bias=nm3[:, i:i + 1],
                                                 accum_out=sum3[:, i:i + 1]).then_inc(sem("pe3"), 1)
                    if s == 12 and on["E"]:
                        act.wait_ge(sem("x1T_pe"), done(t - 1))
                        act.wait_ge(sem("h_pe"), done(t - 2))
                        copy(x1T[0][:], bank["x1T"][:].rearrange("p (c q) -> p c q", c=2)).then_inc(sem("x1Thi"), 1)
                    if s == 13 and on["F"]:
                        act.wait_ge(sem("pT_pe"), done(t - 2))
                        act.wait_ge(sem("pool_pe"), done(t - 3))
                        copy(p3T[:], bank["pT"][:].rearrange("p (c q) -> p c q", c=2)).then_inc(sem("p3T"), 1)
                    if s == 13 and on["B"]:
                        act.wait_ge(sem("vs_pe"), done(t + 1))
                        act.wait_ge(sem("tv"), done(t))
                        copy(vself[:], bank["vs"][:].rearrange("p (c n) -> p c n", c=2)).then_inc(sem("vself"), 1)
                    if s == 14 and on["E"]:
                        act.wait_ge(sem("h_pe"), done(t - 1))
                        act.wait_ge(sem("ad_pe"), done(t - 2))
                        act.wait_ge(sem("ld_b1"), done(t - 1, 32))
                        nc.scalar.activation(hst[:], bank["h"][:, 0:S], ACT.Relu, bias=b1c[:, 0:1]).then_inc(sem("hhi"), 1)

            steps(act, step)

        @block.vector
        def _(dve):
            def wide(n):
                return bank[n][:].rearrange("p (c q) -> p c q", c=2)

            link = sem("set_dve_order")
            n_link = [0]

            def after(ins):
                n_link[0] += 1
                ins.then_inc(link, 1)
                dve.wait_ge(link, n_link[0])

            for i in range(2):
                nc.vector.memset(qst[i][0:96].bitcast(F32), 0.0).then_inc(link, 1)
                nc.vector.memset(qst[i][96:98].bitcast(F32), 1.0).then_inc(link, 1)
                nc.vector.memset(vaug[i][:, :, :, DH + 1:VW], 0.0).then_inc(link, 1)
                nc.vector.memset(vaug[i][:, :, :, DH:DH + 1], 1.0).then_inc(link, 1)
            n_link[0] += 8
            dve.wait_ge(link, n_link[0])
            dve.wait_ge(ld_w, 16 * WL)
            after(nc.vector.tensor_copy(lenf[:], leni[:]))
            nc.vector.tensor_scalar(mrows, kid, lenf[:, 0:1], NEG, ALU.is_ge, ALU.mult).then_inc(sem("mask_split"), 1)
            for n in ("q", "k", "v", "o"):
                after(nc.vector.tensor_copy(W[n][0][:], raw[n]))
                after(nc.vector.tensor_tensor(W[n][1][:], raw[n], W[n][0][:].bitcast(F32), ALU.subtract))
            after(nc.vector.tensor_copy(headsr[:], heads[:]))
            for c in range(NC2):
                nc.vector.tensor_copy(bvb[:, c, :], bcol[:, 8 + c:9 + c].to_broadcast([P, P])).then_inc(set_dve, 1)
            dve.wait_ge(set_pe, 1)
            bias = M[0]
            after(nc.vector.tensor_tensor(bqc[:], bias[:, 0:2], bcol[:, 0:2], ALU.add))
            after(nc.vector.tensor_tensor(bkc[:], bias[:, 2:4], bcol[:, 2:4], ALU.add))
            after(nc.vector.tensor_tensor(bsc[:], bias[:, 4:6], bcol[:, 2:4], ALU.add))
            after(nc.vector.tensor_tensor(bop[:], M[1][:, 0:D], bos, ALU.add))
            nc.vector.tensor_tensor(btab[:, D:NX], M[2][0:SUBJ, 0:A1], b3s, ALU.add).then_inc(sem("btab"), 1)
            for j in range(SUBJ):
                i = j % 2
                dve.wait_ge(ld_l[i], 32 * (j // 2 + 1))
                nc.vector.tensor_tensor(lwn[i], lwn[i], eye2[:], ALU.add).then_inc(eyed, 1)
                after(nc.vector.tensor_tensor(lcat[i][:, :, 0:D], lcat[i][:, :, 0:D], eye2[:], ALU.add))
                dve.wait_ge(fold, j + 1)
                after(nc.vector.tensor_copy(lcat[i][:, :, D:NX],
                                            SN[i][:, 0:2 * A1].rearrange("p (c n) -> p c n", c=NC2)))
                if j >= 2:
                    dve.wait_ge(lsaved, 16 * (j - 1))
                after(nc.vector.tensor_copy(lwst[i][:, 0], lcat[i]))
                nc.vector.tensor_tensor(lwst[i][:, 1], lcat[i], lwst[i][:, 0].bitcast(F32),
                                        ALU.subtract).then_inc(lsplit, 1)
            dve.wait_ge(lsplit, SUBJ)
            dve.wait_ge(lsaved, 16 * SUBJ)
            dve.wait_ge(saved, 32)
            for i in range(2):
                after(nc.vector.memset(kst[i][96:98].bitcast(F32), 1.0))
            nc.vector.memset(rec[:], 0.0).then_inc(ready, 1)
            dve.wait_ge(sem("ld_v3"), 32)

            def step(t, par):
                on = at_work(t)
                odd = 1 - par

                def maxima(half, b, i):
                    hs = slice(8 * half, 8 * half + 8)
                    dve.wait_ge(sem("nself"), done(b))
                    dve.wait_ge(sem("maxed"), before(b, 8 * half + 8))
                    dve.wait_ge(sem(f"m{half}_pe"), done(b - 2))
                    return nc.vector.scalar_tensor_tensor(out=mneg[i][:, :, hs], in0=mx[i][:, :, hs], scalar=-1.0,
                                                          in1=nself[i][:, :, hs], op0=ALU.mult, op1=ALU.min)

                for s in range(UNITS):
                    if s == 0 and on["C"]:
                        maxima(1, t, par).then_inc(sem("mneg1"), 1)
                        dve.wait_ge(sem("mneg1"), done(t))
                        dve.wait_ge(sem("mneg0"), done(t))
                        dve.wait_ge(sem("eself"), done(t - 1))
                        nc.vector.tensor_tensor(earg[:], mneg[par][:].bitcast(F32), nself[par][:],
                                                ALU.subtract).then_inc(sem("earg"), 1)
                    if on["B"]:
                        dve.wait_ge(sem("sn_ready"), before(t + 1, s + 1))
                        if s < 2:
                            dve.wait_ge(sem("earg"), done(t - 1))
                        nc.vector.tensor_reduce(out=mx[odd][:, s % 2, 2 * (s // 2):2 * (s // 2) + 2],
                                                in_=SN[s % 2][:].rearrange("p (h k) -> p h k", h=2),
                                                op=ALU.max, axis=AX.X).then_inc(sem("maxed"), 1)
                    if s == 0 and on["F"]:
                        dve.wait_ge(sem("ad_pe"), done(t - 2))
                        dve.wait_ge(sem("x1b2"), done(t - 2))
                        nc.vector.tensor_tensor(y[:], wide("ad"), x1b2[:], ALU.add).then_inc(sem("y"), 1)
                        dve.wait_ge(sem("y"), done(t - 2))
                        for i in range(2):
                            nc.vector.bn_stats(st[:, i, :], y[:, i, :]).then_inc(sem("st"), 1)
                        dve.wait_ge(sem("st"), done(t - 2, 2))
                        dve.wait_ge(sem("veps"), done(t - 3))
                        dve.sem_inc(sem("waited_dve"), 1)
                        nc.vector.bn_aggr(mv[:, 0, :], st[:, 0, :]).then_inc(sem("va"), 1)
                        nc.vector.bn_aggr(mv[:, 1, :], st[:, 1, :]).then_inc(sem("var"), 1)
                    if s == 1 and on["F"]:
                        dve.wait_ge(sem("rstd"), done(t - 2))
                        dve.wait_ge(sem("x2"), done(t - 3))
                        dve.wait_ge(sem("var"), done(t - 2))
                        dve.wait_ge(sem("va"), done(t - 2))
                        for i in range(2):
                            nc.vector.tensor_scalar(yn[:, i, :], y[:, i, :], mv[:, i, 0:1], rstd[:, i:i + 1],
                                                    ALU.subtract, ALU.mult).then_inc(sem("norm0" if i == 0 else "normed"), 1)
                    if s == 3 and on["F"]:
                        dve.wait_ge(sem("gained"), done(t - 2))
                        dve.wait_ge(sem("x1sum"), done(t - 2))
                        dve.wait_ge(sem("x2T_pe"), done(t - 3))
                        nc.vector.tensor_tensor(x2[:], yg[:], x1be[:], ALU.add).then_inc(sem("x2"), 1)
                    if s == 4 and on["F"]:
                        dve.wait_ge(sem("x2Thi"), done(t - 2))
                        dve.wait_ge(sem("lin"), done(t - 3, 2))
                        nc.vector.tensor_tensor(x2T[1][:], wide("x2T"), x2T[0][:].bitcast(F32),
                                                ALU.subtract).then_inc(sem("x2Tlo"), 1)
                    for i in range(2):
                        if s == 4 + i and on["E"]:
                            v4 = bank[f"num{i}"][:].rearrange("p (h w) -> p h w", w=VW)
                            dve.wait_ge(sem("num_pe"), done(t - 1, 2, i + 1))
                            dve.wait_ge(sem("eself"), done(t - 1))
                            dve.wait_ge(sem("tv"), done(t - 1))
                            dve.wait_ge(sem("aT_pe"), done(t - 2))
                            nc.vector.tensor_tensor(tot[:, i, :], v4[:, :, DH], eself[odd][:, i, :],
                                                    ALU.add).then_inc(sem("tot"), 1)
                            nc.vector.tensor_tensor(nv[:, i, :].rearrange("p (h d) -> p h d", d=DH), v4[:, :, 0:DH],
                                                    tv[odd][:, i, :].rearrange("p (h d) -> p h d", d=DH),
                                                    ALU.add).then_inc(sem("nv"), 1)
                            dve.wait_ge(sem("tot"), done(t - 1, 2, i + 1))
                            nc.vector.reciprocal(rec[:, i, :], tot[:, i, :]).then_inc(sem("rec"), 1)
                        if s == 6 + i and on["F"]:
                            dve.wait_ge(sem("lin"), done(t - 2, 2, i + 1))
                            dve.wait_ge(sem("ld_lb"), done(t - 2, 16))
                            dve.wait_ge(sem("tanh"), done(t - 3))
                            dve.wait_ge(sem("pool_pe"), done(t - 3))
                            dve.wait_ge(sem("outs"), done(t - 3, 2))
                            nc.vector.tensor_tensor(x3[:, i, :], bank[f"lin{i}"][:, 0:NX], lbr[:],
                                                    ALU.add).then_inc(sem("x3"), 1)
                    if s == 8 and on["A"]:
                        dve.wait_ge(sem("ks_pe"), done(t + 2))
                        dve.wait_ge(sem("qf"), done(t + 2))
                        dve.wait_ge(sem("qe"), done(t + 2))
                        dve.wait_ge(sem("psplit"), done(t + 1))
                        for e in range(2):
                            nc.vector.scalar_tensor_tensor(out=pr[:, e, :], in0=bank["ks"][:, e * S:e * S + S],
                                                           scalar=bsc[:, e:e + 1], in1=qf[:, e, :], op0=ALU.add,
                                                           op1=ALU.mult).then_inc(sem("pr0" if e == 0 else "prod"), 1)
                    if s == 8 and on["E"]:
                        dve.wait_ge(sem("aThi"), done(t - 1))
                        dve.wait_ge(sem("wo_pe"), done(t - 2))
                        nc.vector.tensor_tensor(aT[1][:], wide("aT"), aT[0][:].bitcast(F32),
                                                ALU.subtract).then_inc(sem("aTlo"), 1)
                    if s == 8 and on["F"]:
                        dve.wait_ge(sem("tanh"), done(t - 2))
                        dve.wait_ge(sem("sc"), done(t - 3))
                        nc.vector.tensor_tensor(tvv[:], th[:], v3r[:], ALU.mult).then_inc(sem("tvv"), 1)
                        dve.wait_ge(sem("tvv"), done(t - 2))
                        dve.wait_ge(sem("srep_pe"), done(t - 3))
                        nc.vector.tensor_reduce(out=sc[:], in_=tvv[:], op=ALU.add, axis=AX.X).then_inc(sem("sc"), 1)
                    if s == 9 and on["B"]:
                        maxima(0, t + 1, odd).then_inc(sem("mneg0"), 1)
                    if s == 10 and on["E"]:
                        dve.wait_ge(sem("wo_pe"), done(t - 1))
                        dve.wait_ge(sem("xb"), done(t - 1))
                        dve.wait_ge(sem("x1T_pe"), done(t - 2))
                        dve.wait_ge(sem("x1sum"), done(t - 2))
                        dve.wait_ge(sem("x1b2"), done(t - 2))
                        nc.vector.tensor_tensor(x1[:], wide("wo"), xb[:], ALU.add).then_inc(sem("x1"), 1)
                    if s == 10 and on["F"]:
                        dve.wait_ge(sem("srep_pe"), done(t - 2))
                        dve.wait_ge(sem("ld_pm"), done(t - 2, 16))
                        dve.wait_ge(sem("pe3"), done(t - 3, 2))
                        nc.vector.tensor_tensor(msc[:], bank["srep"][:, 0:S].unsqueeze(1).to_broadcast([P, 2, S]),
                                                pm[:, :, 0:S], ALU.add).then_inc(sem("masked"), 1)
                        dve.wait_ge(sem("masked"), done(t - 2))
                        nc.vector.tensor_reduce(out=nm3[:], in_=msc[:], op=ALU.max, axis=AX.X,
                                                negate=True).then_inc(sem("nm3"), 1)
                    if s == 12 and on["E"]:
                        dve.wait_ge(sem("x1Thi"), done(t - 1))
                        dve.wait_ge(sem("h_pe"), done(t - 2))
                        nc.vector.tensor_tensor(x1T[1][:], wide("x1T"), x1T[0][:].bitcast(F32),
                                                ALU.subtract).then_inc(sem("x1Tlo"), 1)
                    if s == 12 and on["A"]:
                        dve.wait_ge(sem("ss_pe"), done(t + 2))
                        dve.wait_ge(sem("earg"), done(t))
                        nc.vector.tensor_scalar(nself[par][:], bank["ss"][:, 0:2 * H].rearrange("p (c h) -> p c h", c=2),
                                                -1.0, None, ALU.mult).then_inc(sem("nself"), 1)
                    if s == 13 and on["F"]:
                        dve.wait_ge(sem("pe3"), done(t - 2, 2))
                        dve.wait_ge(sem("outs"), done(t - 3, 2))
                        nc.vector.tensor_tensor(sc3[:], sum3[:], pm[:, :, S], ALU.mult).then_inc(sem("sc3"), 1)
                        dve.wait_ge(sem("sc3"), done(t - 2))
                        nc.vector.reciprocal(r3[:], sc3[:]).then_inc(sem("r3"), 1)
                    if s == 15 and on["E"]:
                        dve.wait_ge(sem("hhi"), done(t - 1))
                        dve.wait_ge(sem("hlo"), done(t - 2))
                        nc.vector.tensor_scalar(hf[64:128, :], bank["h"][64:128, 0:S], b1c[64:128, 0:1], 0.0,
                                                ALU.add, ALU.max).then_inc(sem("hf"), 1)
                        dve.wait_ge(sem("hf"), done(t - 1))
                        nc.vector.tensor_tensor(hst[64:128, :], hf[64:128, :], hst[64:128, :].bitcast(F32),
                                                ALU.subtract).then_inc(sem("hlo"), 1)
                    if s == 15 and on["F"]:
                        dve.wait_ge(sem("pool_pe"), done(t - 2))
                        dve.wait_ge(sem("r3"), done(t - 2))
                        dve.wait_ge(sem("x3"), done(t - 2, 2))
                        dve.wait_ge(sem(f"stored{par}"), loaded(t - 4, par))
                        for i in range(2):
                            nc.vector.scalar_tensor_tensor(out=ob[par][:, i, :], in0=bank["pool"][:, i * D:i * D + D],
                                                           scalar=r3[:, i:i + 1], in1=x3[:, i, 0:D], op0=ALU.mult,
                                                           op1=ALU.add).then_inc(sem("outs"), 1)

            steps(dve, step)


def kernel(**a):
    import concourse.bacc as bacc
    from concourse.bass_utils import run_bass_kernel_spmd

    def c(v):
        return np.ascontiguousarray(v)

    order = np.array([(2 * (PH * half + p) + e) * DH + d
                      for e in range(2) for half in range(2) for d in range(DH) for p in range(PH)])
    ins = {n: np.asarray(v) for n, v in a.items()}
    col = lambda v: c(v.reshape(NC2, P).T)
    rows = np.arange(S)
    masks = np.stack([rows[None, :] <= rows[:, None], rows[None, :] >= rows[:, None], rows[None, :] != rows[:, None]])
    pmask = np.concatenate([np.where(masks, 0.0, NEG), masks.sum(-1, keepdims=True)], -1).astype(np.float32)
    heads = np.zeros((2 * P, H), np.float32)
    heads[np.arange(2 * P), order // DH] = 1.0
    data = {
        "x": c(ins["x"]), "xT": c(ins["x"].transpose(0, 2, 1)), "sT": c(ins["fside_BxSxS_0"].transpose(0, 2, 1)),
        "lens": c(ins["itok_B_18_1004"].reshape(B, 1)), "lang": c(ins["itok_B_0_8"].reshape(1, B)),
        "subj": c(ins["itok_B_0_7"].reshape(1, B)), "kind": c(ins["itok_B_0_2"].reshape(1, B)),
        "wq": c(ins["L0_cond_Wq"][:, order]), "bq": col(ins["L0_cond_bq"][order]),
        "wk": c(ins["L0_cond_Wk"][:, order]), "bk": col(ins["L0_cond_bk"][order]),
        "wv": c(ins["L0_cond_Wv"]), "bv": col(ins["L0_cond_bv"]),
        "wo": c(ins["L0_cond_Wo"]), "bo": c(ins["L0_cond_bo"].reshape(1, D)),
        "bprev": col(ins["L0_cond_b_prev"].reshape(-1)), "bself": col(ins["L0_cond_b_self"].reshape(-1)),
        "w1": c(ins["L1_cond_W1"]), "b1": c(ins["L1_cond_b1"].reshape(LANG, A1, 1)),
        "w2": c(ins["L1_cond_W2"]), "b2": c(ins["L1_cond_b2"]),
        "gamma": c(ins["L1_cond_gamma"]), "beta": c(ins["L1_cond_beta"]),
        "lw": c(ins["L2_cond_weight"]), "lwT": c(ins["L2_cond_weight"].transpose(0, 2, 1)),
        "lb": c(ins["L2_cond_bias"]), "lbT": c(ins["L2_cond_bias"].T),
        "w3": c(ins["L3_cond_W1"]), "b3": c(ins["L3_cond_b1"].reshape(1, A1)), "v3": c(ins["L3_cond_v"].reshape(1, A1)),
        "ident": np.eye(P, dtype=np.float32), "eye2": np.eye(D, dtype=np.float32),
        "heads": c(heads.reshape(2, P, H).transpose(1, 0, 2)),
        "kidx": np.tile(np.arange(S, dtype=np.float32), (B, 1)), "pmask": pmask,
    }
    nc = bacc.Bacc("TRN2", target_bir_lowering=False, num_devices=1)
    aps = [nc.dram_tensor(f"in_{n}", v.shape, mybir.dt.from_np(v.dtype), kind="ExternalInput").ap()
           for n, v in data.items()]
    o = nc.dram_tensor("out_0", (B, S, D), F32, kind="ExternalOutput").ap()
    by = dict(zip(data, aps))
    block4(nc, by["x"], by["xT"], by["sT"], by["lens"], by["lang"], by["subj"], by["kind"], by["wq"], by["bq"],
           by["wk"], by["bk"], by["wv"], by["bv"], by["wo"], by["bo"], by["bprev"], by["bself"], by["w1"], by["b1"],
           by["w2"], by["b2"], by["gamma"], by["beta"], by["lw"], by["lwT"], by["lb"], by["lbT"], by["w3"], by["b3"],
           by["v3"], by["ident"], by["eye2"], by["heads"], by["kidx"], by["pmask"], o)
    r = run_bass_kernel_spmd(nc, [{f"in_{n}": v for n, v in data.items()}], core_ids=[0])
    return r.results[0]["out_0"]
```

```python
from contextlib import ExitStack

import numpy as np
import concourse.bass as bass
from concourse import mybir

F32 = mybir.dt.float32
F32R = mybir.dt.float32r
I32 = mybir.dt.int32
ALU = mybir.AluOpType
ACT = mybir.ActivationFunctionType
AX = mybir.AxisListType

B, S, D = 32, 256, 256
H, DH = 16, 16
P = 128
NC2 = D // P
PAIRS = H // 2
PH = PAIRS // 2
A1 = 64
LANG, SUBJ, KINDS = 10, 8, 3
VW = 32
NX = D + A1
NEG = -1e30
EPS = 1e-5
SCALE = 1.0 / 4.0
UNITS = 16
SPLIT = ((0, 0), (0, 1), (1, 0))
SK = 16 * (2 * (3 + 3) + 1)
FIRST, LAST = 6, 28

PIECES = [
    (0, "ks", 1, 1), (0, "m1", 0, 0), (1, "pv1", -1, 3), (1, "h", -2, 2), (3, "q", 2, 3),
    (3, "num0", -1, 1), (3, "srep", -3, 0), (4, "num1", -1, 2), (5, "pv0", 0, 3), (5, "ad", -2, 0),
    (6, "k", 2, 2), (7, "pT", -3, 0), (8, "ss", 1, 1), (8, "v", 1, 2), (9, "aT", -1, 1),
    (10, "pool", -3, 0), (10, "m0", 1, 2), (11, "x2T", -2, 3), (11, "wo", -1, 1), (12, "vs", 1, 2),
    (13, "pv1", 0, 3), (14, "lin0", -2, 0), (14, "x1T", -1, 1), (15, "lin1", -2, 2),
]
NAMES = [n for _, n, _, _ in PIECES]


def done(b, per=1, nth=None):
    nth = per if nth is None else nth
    if isinstance(b, int):
        return 0 if b < 0 else B * per if b >= B else b * per + nth
    return b * per + nth


def loaded(b, par):
    return max(0, 8 * (b - par) + 16) if isinstance(b, int) else 8 * (b - par) + 16


def before(b, unit):
    if isinstance(b, int):
        return max(0, min(b, B) * UNITS + unit) if b < B else B * UNITS
    return b * UNITS + unit


def block4(nc: bass.Bass, x, xsT, lens, lang, subj, kind, wq, bq, wk, bk, wv, bv, wo, bo, bprev,
           bself, wad, b2, gamma, beta, lw, lwT, lb, lbT, w3, b3, v3, ident_d, eye2_d,
           heads_d, kidx_d, pmask_d, out):
    ctx = ExitStack()
    with ctx:
        def sb(name, shape, dt=F32):
            return ctx.enter_context(nc.sbuf_tensor(name, shape, dt))

        def pb(name):
            return ctx.enter_context(nc.psum_tensor(name, [P, 512], F32))

        sems = {}

        def sem(name):
            if name not in sems:
                sems[name] = ctx.enter_context(nc.semaphore(name))
            return sems[name]

        qst = [sb(f"qst{i}", [P, PAIRS, 2 * S], F32R) for i in range(2)]
        kst = [sb(f"kst{i}", [P, PAIRS, S], F32R) for i in range(2)]
        xsin = [sb(f"xsin{i}", [P, 2, NC2, S]) for i in range(2)]
        xin, sin = [a[:, 0] for a in xsin], [a[:, 1] for a in xsin]
        xs = [[sb(f"xs{i}{r}", [P, NC2, S], F32R) for r in range(2)] for i in range(2)]
        ss = [[sb(f"ss{i}{r}", [P, NC2, S], F32R) for r in range(2)] for i in range(2)]
        qf = sb("qf", [P, 2, S])
        kf = sb("kf", [P, 2, S])
        pr = sb("pr", [P, 2, S])
        qp = [sb(f"qp{r}", [P, 2, S], F32R) for r in range(2)]
        kp = [sb(f"kp{r}", [P, 2, S], F32R) for r in range(2)]
        pp = [sb(f"pp{r}", [P, 2, S], F32R) for r in range(2)]
        nself = [sb(f"nself{i}", [P, 2, H]) for i in range(2)]
        mx = [sb(f"mx{i}", [P, 2, H]) for i in range(2)]
        mneg = [sb(f"mneg{i}", [P, 2, H], F32R) for i in range(2)]
        mrow = sb("mrow", [PAIRS, 2, P], F32R)
        earg = sb("earg", [P, 2, H])
        eself = [sb(f"eself{i}", [P, 2, H]) for i in range(2)]
        vaug = [sb(f"vaug{i}", [P, 2, H, VW]) for i in range(2)]
        vself = sb("vself", [P, 2, D])
        tv = [sb(f"tv{i}", [P, 2, D]) for i in range(2)]
        pt = sb("pt", [P, 2, 2, 4, S])
        pvt = sb("pvt", [P, 4, S])
        tot = sb("tot", [P, 2, H])
        rec = sb("rec", [P, 2, H])
        nv = sb("nv", [P, 2, D])
        att = nv
        aT = [sb(f"aT{r}", [P, NC2, S], F32R) for r in range(2)]
        xr = sb("xr", [P, 2, D])
        xb = xr
        x1 = sb("x1", [P, 2, D])
        x1b2 = sb("x1b2", [P, 2, D])
        x1be = sb("x1be", [P, 2, D])
        x1T = [sb(f"x1T{r}", [P, NC2, S], F32R) for r in range(2)]
        adw = sb("adw", [P, NC2 * A1 + D + 1])
        w1raw = adw[:, 0:NC2 * A1].rearrange("p (c n) -> p c n", c=NC2)
        w2raw = adw[:, NC2 * A1:NC2 * A1 + D]
        b1c = adw[:, NC2 * A1 + D:NC2 * A1 + D + 1]
        w1p = [sb(f"w1p{r}", [P, NC2, 2, A1], F32R) for r in range(2)]
        w2p = [sb(f"w2p{r}", [P, D], F32R) for r in range(2)]
        b2r = sb("b2r", [P, D])
        gar = sb("gar", [P, D])
        ber = sb("ber", [P, D])
        hst = sb("hst", [P, S], F32R)
        hf = sb("hf", [P, S])
        y = sb("y", [P, 2, D])
        st = sb("st", [P, 2, 6])
        mv = sb("mv", [P, 2, 2])
        veps = sb("veps", [P, 2])
        rstd = sb("rstd", [P, 2])
        mhalf = sb("mhalf", [P, 2])
        yn = sb("yn", [P, 2, D])
        yg = yn
        x2 = sb("x2", [P, 2, D])
        x2T = [sb(f"x2T{r}", [P, NC2, S], F32R) for r in range(2)]
        lwp = sb("lwp", [P, 2, NC2, NX], F32R)
        lbr = sb("lbr", [P, NX])
        x3 = sb("x3", [P, 2, NX])
        th = sb("th", [P, 2, A1])
        v3r = sb("v3r", [P, 2, A1])
        tvv = sb("tvv", [P, 2, A1])
        sc = sb("sc", [P, 2])
        pm = sb("pm", [P, 2, S + 1])
        msc = sb("msc", [P, 2, S])
        nm3 = sb("nm3", [P, 2])
        pe3 = sb("pe3", [P, 2, S])
        sum3 = sb("sum3", [P, 2])
        sc3 = sb("sc3", [P, 2])
        r3 = sb("r3", [P, 2])
        p3T = sb("p3T", [P, 2, S])
        ob = [sb(f"ob{i}", [P, 2, D]) for i in range(2)]
        W = {n: [sb(f"W{n}{r}", [P, NC2, D], F32R) for r in range(2)] for n in ("q", "k", "v", "o")}
        ident = sb("ident", [P, P])
        headsr = sb("headsr", [P, 2, H], F32R)
        heads = sb("heads", [P, 2, H])
        bqc = sb("bqc", [P, 2])
        bkc = sb("bkc", [P, 2])
        bsc = sb("bsc", [P, 2])
        bop = sb("bop", [P, D])
        idx = sb("idx", [1, 3, B], I32)
        flat = pt[:, :, :, :, :].rearrange("p a b c d -> p (a b c d)")
        raw = {n: flat[:, 512 * i:512 * i + 512].rearrange("p (c n) -> p c n", c=NC2)
               for i, n in enumerate(("q", "k", "v", "o"))}
        lwn = [flat[:, 2048 + 512 * i:2560 + 512 * i].rearrange("p (c n) -> p c n", c=NC2) for i in range(2)]
        lcat = [flat[:, at:at + NC2 * NX].rearrange("p (c n) -> p c n", c=NC2) for at in (3072, 0, NC2 * NX)]
        lcat.insert(1, x3[:, :, :])
        NCAT = len(lcat)
        eye2 = y
        w3s = x1b2[:, 0, 0:2 * A1].rearrange("p (c n) -> p c n", c=NC2)
        bvb = x1[:, :, 0:P]
        bcol = msc[:, 0, 0:16]
        lbTs = msc[:, 1, 0:16].rearrange("p (c s) -> p c s", c=NC2)
        btab = tv[0][0:SUBJ, :, :].rearrange("p a b -> p (a b)")[:, 0:NX]
        b3s = att[0:SUBJ, 1, 0:A1]
        bos = x1be[:, 0, :]
        kid = yn[0:B, 0, :]
        mrows = hst[0:B, :]
        lenf = sb("lenf", [B, 1])
        leni = sb("leni", [B, 1], I32)

        SN = [pb(f"SN{i}") for i in range(2)]
        ST = [pb(f"ST{i}") for i in range(2)]
        PV = pb("PV")
        M = [pb(f"M{i}") for i in range(3)]
        bank = {n: M[k] for _, n, _, k in PIECES if k < 3} | {"q": PV, "x2T": PV}

        lws_d = nc.dram_tensor("lws", [SUBJ, P, 2 * NC2 * NX], F32, kind="Internal").ap()
        lbs_d = nc.dram_tensor("lbs", [SUBJ, NX], F32, kind="Internal").ap()
        mrow_d = nc.dram_tensor("mrows", [B, S], F32, kind="Internal").ap()

        lwst = [lwp[:, :, :, :], kst[1][:, :, :].rearrange("p a n -> p (a n)")[:, 0:2 * NC2 * NX].rearrange(
            "p (r c n) -> p r c n", r=2, c=NC2)]
        xsT3 = xsT.rearrange("b a (c p) n -> b p a c n", p=P)
        x4, o4 = (a.rearrange("b (c p) n -> b p c n", p=P) for a in (x, out))
        pm3 = pmask_d.rearrange("k (c p) n -> k p c n", p=P)

        ld_w = sem("ld_w")
        ld_ln = [sem(f"ld_ln{i}") for i in range(2)]
        ld_lc = [sem(f"ld_lc{i}") for i in range(4)]
        set_dve = sem("set_dve")
        set_pe = sem("set_pe")
        set_act = sem("set_act")
        fold = sem("fold")
        cat = sem("cat")
        eyed = sem("eyed")
        eyec = sem("eyec")
        lhi = sem("lhi")
        lsplit = sem("lsplit")
        lsaved = [sem("lsaved0"), sem("lsaved1")]
        saved = sem("saved")
        ready = sem("ready")
        tables = sem("tables")

        block = ctx.enter_context(nc.Block())
        WL = 19

        def at_work(t):
            if not isinstance(t, int):
                return dict.fromkeys("ABCEFG", True)
            return {n: 0 <= t + o < B for n, o in zip("ABCEFG", (2, 1, 0, -1, -2, -3))}

        def steps(eng, step):
            step(-1, 1)
            eng.wait_ge(tables, 1)
            for t in range(0, FIRST):
                step(t, t % 2)
            with eng.Fori(FIRST, LAST, 2) as t:
                step(t, 0)
                step(t + 1, 1)
            for t in range(LAST, B + 3):
                step(t, t % 2)

        def tokens(a):
            return a.rearrange("(c p) n -> p c n", p=P)

        @block.sync
        def _(sp):
            loads = [(raw["q"], tokens(wq)), (raw["k"], tokens(wk)), (raw["v"], tokens(wv)),
                     (raw["o"], tokens(wo)), (ident[:], ident_d), (eye2[:], tokens(eye2_d)),
                     (heads[:], heads_d), (bcol[:, 0:2], bq), (bcol[:, 2:4], bk), (bcol[:, 4:6], bself),
                     (bcol[:, 6:8], bprev), (bcol[:, 8:10], bv), (bos, bo.to_broadcast([P, D])),
                     (w3s, tokens(w3)), (lbTs, tokens(lbT)), (kid, kidx_d), (leni[:], lens),
                     (btab[:, 0:D], lb), (b3s, b3.to_broadcast([SUBJ, A1]))]
            assert len(loads) == WL
            with nc.allow_non_contiguous_dma(reason="small constants"):
                for dst, src in loads:
                    sp.dma_start(dst, src).then_inc(ld_w, 16)
            sp.dma_start(idx[:, 0, :], lang).then_inc(sem("ld_i"), 16)
            sp.dma_start(idx[:, 1, :], subj).then_inc(sem("ld_i"), 16)
            sp.dma_start(idx[:, 2, :], kind).then_inc(sem("ld_i"), 16)
            for i in range(2):
                sp.dma_start(v3r[:, i, :], v3.to_broadcast([P, A1])).then_inc(sem("ld_v3"), 16)
            for b in range(2):
                sp.dma_start(xsin[b][:], xsT3[b]).then_inc(sem(f"ld_xs{b}"), 16)

            def load_other(j):
                sp.dma_start(lcat[j % NCAT][:, :, 0:D], tokens(lwT[j])).then_inc(ld_lc[j % NCAT], 16)

            for j in range(2):
                sp.dma_start(lwn[j], tokens(lw[j])).then_inc(ld_ln[j], 16)
                load_other(j)
            sp.wait_ge(sem("mask_split"), 1)
            sp.dma_start(mrow_d, mrows.bitcast(F32)).then_inc(saved, 16)
            sp.wait_ge(sem("btab"), 1)
            sp.dma_start(lbs_d, btab).then_inc(saved, 16)
            def which(k, b, most):
                return sp.value_load(idx[0:1, k, bass.ds(b, 1)], min_val=0, max_val=most)

            def stack_q(half, b, par):
                at, pairs = slice(64 * half, 64 * half + 64), slice(PH * half, PH * half + PH)
                sp.wait_ge(saved, 32)
                sp.wait_ge(sem("qsplit"), done(b))
                sp.wait_ge(sem("st_ready"), done(b - 2, UNITS, UNITS // 2 * (1 + half)))
                for e in range(2):
                    for r in range(3):
                        row = 48 * e + 16 * r
                        sp.dma_start(qst[par][row:row + 16, pairs, e * S:e * S + S].bitcast(F32),
                                     qp[r % 2][at, e, :].bitcast(F32)).then_inc(sem(f"stack{half}"), 16)
                sp.dma_start(kst[par][96:97, pairs, :].bitcast(F32),
                             mrow_d[bass.ds(b, 1), :].unsqueeze(1).to_broadcast([1, PH, S])).then_inc(
                                 sem(f"stack{half}"), 16)

            def stack_k(half, b, par):
                at, pairs = slice(64 * half, 64 * half + 64), slice(PH * half, PH * half + PH)
                sp.wait_ge(saved, 32)
                sp.wait_ge(sem("ksplit"), done(b))
                for e in range(2):
                    for r in range(3):
                        row = 48 * e + 16 * r
                        sp.dma_start(kst[par][row:row + 16, pairs, :].bitcast(F32),
                                     kp[r // 2][at, e, :].bitcast(F32)).then_inc(sem(f"stack{half}"), 16)

            def step(t, par):
                on = at_work(t)
                odd = 1 - par
                if on["B"] and not (isinstance(t, int) and t == -1):
                    stack_q(1, t + 1, odd)
                    stack_k(1, t + 1, odd)
                if on["C"]:
                    sp.wait_ge(saved, 32)
                    sp.wait_ge(sem("mrow1"), done(t))
                    sp.dma_start(qst[par][97:98, PH:PAIRS, :].bitcast(F32), mrow[:, :, :].bitcast(F32)).then_inc(sem("mput1"), 16)
                if not isinstance(t, int) or 2 <= t + 3 < B:
                    sp.wait_ge(saved, 32)
                    sp.wait_ge(sem("xsplit"), done(t + 1))
                    sp.wait_ge(sem("ssplit"), done(t + 1))
                    sp.dma_start(xsin[odd][:], xsT3[t + 3]).then_inc(sem(f"ld_xs{odd}"), 16)
                if on["E"]:
                    la = which(0, t - 1, LANG - 1)
                    sp.wait_ge(saved, 32)
                    sp.wait_ge(sem("wsplit"), done(t - 2))
                    sp.wait_ge(sem("hlo"), done(t - 2))
                    sp.dma_start(adw[:], wad[la]).then_inc(sem("ld_wad"), 16)
                if on["F"]:
                    su = which(1, t - 2, SUBJ - 1)
                    sp.wait_ge(saved, 32)
                    sp.wait_ge(sem("lin"), done(t - 3, 2))
                    sp.dma_start(lwp[:].rearrange("p a b n -> p (a b n)").bitcast(F32), lws_d[su]).then_inc(sem("ld_lw"), 16)
                    sp.wait_ge(sem("x3"), done(t - 3, 2))
                    sp.dma_start(lbr[:], lbs_d[bass.ds(su, 1), :].to_broadcast([P, NX])).then_inc(sem("ld_lb"), 16)
                if on["F"]:
                    ki = which(2, t - 2, KINDS - 1)
                    sp.wait_ge(saved, 32)
                    sp.wait_ge(sem("masked"), done(t - 3))
                    sp.wait_ge(sem("r3"), done(t - 3))
                    sp.dma_start(pm[:], pm3[ki]).then_inc(sem("ld_pm"), 16)
                if on["A"]:
                    stack_q(0, t + 2, par)
                if on["B"]:
                    sp.wait_ge(saved, 32)
                    sp.wait_ge(sem("mrow0"), done(t + 1))
                    sp.dma_start(qst[odd][97:98, 0:PH, :].bitcast(F32), mrow[:, :, :].bitcast(F32)).then_inc(sem("mput0"), 16)
                if on["A"]:
                    stack_k(0, t + 2, par)
                if on["F"]:
                    sp.wait_ge(saved, 32)
                    sp.wait_ge(sem("gained"), done(t - 2))
                if on["E"]:
                    sp.dma_start(gar[:], gamma[bass.ds(la, 1), :].to_broadcast([P, D])).then_inc(sem("ld_ga"), 16)
                if on["G"]:
                    sp.wait_ge(saved, 32)
                    sp.wait_ge(sem("outs"), done(t - 3, 2))
                    sp.dma_start(o4[t - 3], ob[odd][:]).then_inc(sem(f"stored{odd}"), 16)
                if on["C"]:
                    lb_ = which(0, t, LANG - 1)
                    sp.wait_ge(saved, 32)
                    sp.wait_ge(sem("x1"), done(t - 1))
                    sp.dma_start(xr[:], x4[t]).then_inc(sem("ld_xr"), 16)
                    sp.wait_ge(sem("x1sum"), done(t - 1))
                    sp.dma_start(b2r[:], b2[bass.ds(lb_, 1), :].to_broadcast([P, D])).then_inc(sem("ld_b"), 16)
                    sp.dma_start(ber[:], beta[bass.ds(lb_, 1), :].to_broadcast([P, D])).then_inc(sem("ld_b"), 16)

            sp.wait_ge(ready, 1)
            load_other(2)
            load_other(3)
            for j in range(SUBJ):
                if j + 2 < SUBJ:
                    sp.wait_ge(fold, j + 1)
                    sp.dma_start(lwn[j % 2], tokens(lw[j + 2])).then_inc(ld_ln[j % 2], 16)
                sp.wait_ge(lsplit, j + 1)
                sp.wait_ge(lhi, j + 1)
                sp.dma_start(lws_d[j], lwst[j % 2].rearrange("p a b n -> p (a b n)").bitcast(F32)).then_inc(lsaved[j % 2], 16)
                if j + NCAT < SUBJ:
                    load_other(j + NCAT)
                if j in (2, 4):
                    stack_q(j // 2 - 1, 0, 0)
                if j in (3, 5):
                    stack_k(j // 2 - 1, 0, 0)
            for i in range(2):
                sp.wait_ge(lsaved[i], 16 * SUBJ // 2)
            sp.wait_ge(sem("ld_i"), 48)
            sp.wait_ge(tables, 1)
            steps(sp, step)
            for i in range(2):
                sp.wait_ge(sem(f"stored{i}"), 16 * B // 2)


        @block.tensor
        def _(pe):
            def three(dst, left, right):
                n = 0
                for c in range(NC2):
                    for a, b in SPLIT:
                        last = nc.tensor.matmul(dst, left(a, c), right(b, c), start=n == 0, stop=n == 5)
                        n += 1
                return last

            def turn(dst, src):
                for c in range(NC2):
                    for i in range(2):
                        last = nc.tensor.transpose(dst[:, c * S + i * P:c * S + i * P + P],
                                                   src[:, i, c * P:c * P + P], ident[:])
                return last

            pe.wait_ge(ld_w, 16 * WL)
            for n, w, col in ((0, "q", 4), (2, "k", 6), (4, "k", 4)):
                for e in range(2):
                    for c in range(NC2):
                        nc.tensor.matmul(M[0][:, n + e:n + e + 1], raw[w][:, c, e * P:e * P + P],
                                         bcol[:, col + c:col + c + 1], start=c == 0, stop=c == 1)
            pe.wait_ge(set_dve, 2)
            for c in range(NC2):
                nc.tensor.matmul(M[1][:, 0:D], bvb[:, c, :], raw["o"][:, c, :], start=c == 0, stop=c == 1)
            for c in range(NC2):
                last = nc.tensor.matmul(M[2][0:SUBJ, 0:A1], lbTs[:, c, 0:SUBJ], w3s[:, c, :],
                                        start=c == 0, stop=c == 1)
            last.then_inc(set_pe, 1)
            READER = {"q": ("qf", 1, 1), "k": ("kf", 1, 1), "ks": ("prod", 1, 1), "v": ("v", 1, 1),
                      "vs": ("vself", 1, 1), "ss": ("nself", 1, 1), "m0": ("mrow0", 1, 1),
                      "m1": ("mrow1", 1, 1), "num0": ("nv", 2, 1), "num1": ("nv", 2, 2),
                      "aT": ("aTlo", 1, 1), "wo": ("x1", 1, 1), "x1T": ("x1Tlo", 1, 1), "h": ("hlo", 1, 1),
                      "ad": ("y", 1, 1), "x2T": ("x2Tlo", 1, 1), "lin0": ("x3", 2, 1), "lin1": ("x3", 2, 2),
                      "srep": ("masked", 1, 1), "pT": ("p3T", 1, 1), "pool": ("outs", 2, 2),
                      "pv0": ("pvt", 2, 1), "pv1": ("pvt", 2, 2)}

            def step(t, par):
                on = at_work(t)
                odd = 1 - par

                def free(name):
                    k = NAMES.index(name)
                    mine, u = PIECES[k][3], t
                    while True:
                        k -= 1
                        if k < 0:
                            k, u = len(PIECES) - 1, u - 1
                        if isinstance(u, int) and u < -2:
                            return
                        _, n, o, on_bank = PIECES[k]
                        if on_bank == mine and (not isinstance(u, int) or 0 <= u + o < B):
                            if n == "pv1" and o == 0:
                                continue
                            s, per, nth = READER[n]
                            pe.wait_ge(sem(s), done(u + o, per, nth))
                            return

                def group(g, b, i):
                    pe.wait_ge(sem("exp_done"), before(b, 4 * g + 4))
                    pe.wait_ge(sem("v"), done(b))
                    if g == 0:
                        free("pv0")
                    if g == 2:
                        pe.wait_ge(sem("pvt"), done(b, 2, 1))
                        pe.wait_ge(sem("x2Tlo"), done(b - 2))
                    for kb in range(2):
                        for j in range(4):
                            last = nc.tensor.matmul(PV[32 * j:32 * j + 32, (g % 2) * S:(g % 2) * S + S],
                                                    vaug[i][:, kb, 4 * g + j, :], pt[:, g % 2, kb, j, :],
                                                    start=kb == 0, stop=kb == 1)
                    last.then_inc(sem("pv_done"), 1)

                def unit(s):
                    pair, half = s // 2, s % 2
                    if on["C"]:
                        if s == 0 or s == UNITS // 2:
                            pe.wait_ge(sem(f"mput{s // 8}"), done(t, 16))
                        pe.wait_ge(sem("exp_done"), before(t, s - 1) if s else before(t - 1, UNITS - 1))
                        nc.tensor.matmul(ST[s % 2][:], kst[par][0:98, pair, half * P:half * P + P],
                                         qst[par][0:98, pair, :], start=True, stop=True).then_inc(sem("st_ready"), 1)
                    if on["B"]:
                        if s == 0 or s == UNITS // 2:
                            pe.wait_ge(sem(f"stack{s // 8}"), done(t + 1, SK))
                        pe.wait_ge(sem("maxed"), before(t + 1, s - 1) if s else before(t, UNITS - 1))
                        for e in range(2):
                            last = nc.tensor.matmul(SN[s % 2][:, e * S:e * S + S],
                                                    qst[odd][0:97, pair, e * S + half * P:e * S + half * P + P],
                                                    kst[odd][0:97, pair, :], start=True, stop=True)
                        last.then_inc(sem("sn_ready"), 1)

                def rows_of_maxima(half, b, i):
                    free(f"m{half}")
                    pe.wait_ge(sem(f"mneg{half}"), done(b))
                    for c in range(2):
                        last = nc.tensor.transpose(bank[f"m{half}"][0:8, c * P:c * P + P],
                                                   mneg[i][:, c, 8 * half:8 * half + 8].bitcast(F32), ident[:])
                    last.then_inc(sem(f"m{half}_pe"), 1)

                def project(name, w, src):
                    for e in range(2):
                        last = three(bank[name][:, e * S:e * S + S], lambda r, c: w[r][:, c, e * P:e * P + P],
                                     lambda r, c: src[r][:, c, :])
                    last.then_inc(sem(f"{name}_pe"), 1)

                def values(name, left, w):
                    for i in range(2):
                        last = three(bank[name][:, i * D:i * D + D], lambda r, c: left[r][:, c, i * P:i * P + P],
                                     lambda r, c: w[r][:, c, :])
                    last.then_inc(sem(f"{name}_pe"), 1)

                def queries_back(i):
                    free(f"num{i}")
                    pe.wait_ge(sem("pvt"), done(t - 1, 2))
                    for g in range(4):
                        last = nc.tensor.transpose(bank[f"num{i}"][:, g * P:g * P + P],
                                                   pvt[:, g, i * P:i * P + P], ident[:])
                    last.then_inc(sem("num_pe"), 1)

                def linear(i):
                    free(f"lin{i}")
                    pe.wait_ge(sem("x2Thi"), done(t - 2))
                    pe.wait_ge(sem("x2Tlo"), done(t - 2))
                    pe.wait_ge(sem("ld_lw"), done(t - 2, 16))
                    three(bank[f"lin{i}"][:, 0:NX], lambda r, c: x2T[r][:, c, i * P:i * P + P],
                          lambda r, c: lwp[:, r, c, :]).then_inc(sem("lin"), 1)

                unit(0)
                if on["B"]:
                    free("ks")
                    project("ks", W["k"], ss[odd])
                if on["C"]:
                    rows_of_maxima(1, t, par)
                unit(1)
                if on["E"]:
                    group(3, t - 1, odd)
                if on["F"]:
                    free("h")
                    pe.wait_ge(sem("x1Thi"), done(t - 2))
                    pe.wait_ge(sem("x1Tlo"), done(t - 2))
                    pe.wait_ge(sem("wlo"), done(t - 2))
                    pe.wait_ge(sem("wsplit"), done(t - 2))
                    three(bank["h"][:, 0:S], lambda r, c: w1p[r][:, c, :, :].rearrange("p a n -> p (a n)"),
                          lambda r, c: x1T[r][:, c, :]).then_inc(sem("h_pe"), 1)
                unit(2)
                unit(3)
                if on["A"]:
                    free("q")
                    pe.wait_ge(sem("shi"), done(t + 2))
                    pe.wait_ge(sem("ssplit"), done(t + 2))
                    project("q", W["q"], ss[par])
                if on["E"]:
                    queries_back(0)
                if on["G"]:
                    free("srep")
                    pe.wait_ge(sem("sc"), done(t - 3))
                    for i in range(2):
                        last = nc.tensor.transpose(bank["srep"][:, i * P:i * P + P],
                                                   sc[:, i:i + 1].to_broadcast([P, P]), ident[:])
                    last.then_inc(sem("srep_pe"), 1)
                unit(4)
                if on["E"]:
                    queries_back(1)
                unit(5)
                if on["C"]:
                    group(0, t, par)
                if on["F"]:
                    free("ad")
                    pe.wait_ge(sem("hhi"), done(t - 2))
                    pe.wait_ge(sem("hlo"), done(t - 2))
                    for i in range(2):
                        for r in range(2):
                            last = nc.tensor.matmul(bank["ad"][:, i * D:i * D + D], hst[:, i * P:i * P + P],
                                                    w2p[r][:], start=r == 0, stop=r == 1)
                    last.then_inc(sem("ad_pe"), 1)
                unit(6)
                if on["A"]:
                    free("k")
                    pe.wait_ge(sem("xhi"), done(t + 2))
                    pe.wait_ge(sem("xsplit"), done(t + 2))
                    project("k", W["k"], xs[par])
                unit(7)
                if on["G"]:
                    free("pT")
                    pe.wait_ge(sem("pe3"), done(t - 3, 2))
                    turn(bank["pT"], pe3).then_inc(sem("pT_pe"), 1)
                unit(8)
                if on["B"]:
                    free("ss")
                    pe.wait_ge(sem("phi"), done(t + 1))
                    pe.wait_ge(sem("psplit"), done(t + 1))
                    for i in range(2):
                        n = 0
                        for e in range(2):
                            for r in range(2):
                                last = nc.tensor.matmul(bank["ss"][:, i * H:i * H + H],
                                                        pp[r][:, e, i * P:i * P + P], headsr[:, e, :],
                                                        start=n == 0, stop=n == 3)
                                n += 1
                    last.then_inc(sem("ss_pe"), 1)
                if on["B"]:
                    free("v")
                    values("v", xs[odd], W["v"])
                unit(9)
                if on["E"]:
                    free("aT")
                    pe.wait_ge(sem("att"), done(t - 1))
                    turn(bank["aT"], att).then_inc(sem("aT_pe"), 1)
                if on["C"]:
                    group(1, t, par)
                unit(10)
                if on["G"]:
                    free("pool")
                    pe.wait_ge(sem("p3T"), done(t - 3))
                    for i in range(2):
                        for c in range(2):
                            last = nc.tensor.matmul(bank["pool"][:, i * D:i * D + D], p3T[:, c, i * P:i * P + P],
                                                    x3[:, c, 0:D], start=c == 0, stop=c == 1)
                    last.then_inc(sem("pool_pe"), 1)
                if on["B"]:
                    rows_of_maxima(0, t + 1, odd)
                unit(11)
                if on["F"]:
                    free("x2T")
                    pe.wait_ge(sem("x2"), done(t - 2))
                    turn(bank["x2T"], x2).then_inc(sem("x2T_pe"), 1)
                if on["E"]:
                    free("wo")
                    pe.wait_ge(sem("aThi"), done(t - 1))
                    pe.wait_ge(sem("aTlo"), done(t - 1))
                    values("wo", aT, W["o"])
                unit(12)
                if on["B"]:
                    free("vs")
                    values("vs", ss[odd], W["v"])
                unit(13)
                if on["C"]:
                    group(2, t, par)
                unit(14)
                if on["F"]:
                    linear(0)
                if on["E"]:
                    free("x1T")
                    pe.wait_ge(sem("x1"), done(t - 1))
                    turn(bank["x1T"], x1).then_inc(sem("x1T_pe"), 1)
                unit(15)
                if on["F"]:
                    linear(1)

            for j in range(SUBJ):
                i = j % 2
                if j == 2:
                    pe.wait_ge(ready, 1)
                    step(-2, 0)
                pe.wait_ge(eyed, j + 1)
                if j >= 2:
                    pe.wait_ge(cat, j - 1)
                for hc in range(NC2):
                    for oc in range(NC2):
                        last = nc.tensor.matmul(SN[i][:, hc * A1:hc * A1 + A1], lwn[i][:, oc, hc * P:hc * P + P],
                                                w3s[:, oc, :], start=oc == 0, stop=oc == 1)
                last.then_inc(fold, 1)
            pe.wait_ge(cat, SUBJ)
            steps(pe, step)

        @block.gpsimd
        def _(pool):
            fixed = ((qst[1][0:96].bitcast(F32), 0.0), (kst[0][96:98].bitcast(F32), 1.0),
                     (qst[0][96:98].bitcast(F32), 1.0), (qst[1][96:98].bitcast(F32), 1.0), (mhalf[:], -0.5))
            for n, (part, value) in enumerate(fixed):
                nc.gpsimd.memset(part, value).then_inc(sem("pool_set"), 1)
                pool.wait_ge(sem("pool_set"), n + 1)

            def hi(dst, src):
                pool.sem_inc(sem("waited_pool"), 1)
                return nc.gpsimd.tensor_scalar(dst, src, 1.0, 0.0, ALU.mult, ALU.add)

            def lo(dst, src, high):
                return nc.gpsimd.tensor_tensor(dst, src, high.bitcast(F32), ALU.subtract)

            def step(t, par):
                on = at_work(t)
                if on["A"]:
                    pool.wait_ge(sem("shi"), done(t + 2))
                    pool.wait_ge(sem("vs_pe"), done(t))
                    lo(ss[par][1][:], sin[par], ss[par][0][:]).then_inc(sem("ssplit"), 1)
                if on["B"]:
                    pool.wait_ge(sem("prod"), done(t + 1))
                    pool.wait_ge(sem("ss_pe"), done(t))
                    hi(pp[0][:], pr[:]).then_inc(sem("phi"), 1)
                    pool.wait_ge(sem("phi"), done(t + 1))
                    lo(pp[1][:], pr[:], pp[0][:]).then_inc(sem("psplit"), 1)
                if on["A"]:
                    pool.wait_ge(sem("xhi"), done(t + 2))
                    pool.wait_ge(sem("v_pe"), done(t))
                    lo(xs[par][1][:], xin[par], xs[par][0][:]).then_inc(sem("xsplit"), 1)
                if on["E"]:
                    pool.wait_ge(sem("nv"), done(t - 1, 2))
                    pool.wait_ge(sem("rec"), done(t - 1, 2))
                    nc.gpsimd.tensor_tensor(att[:].rearrange("p c (h d) -> p c h d", d=DH),
                                            nv[:].rearrange("p c (h d) -> p c h d", d=DH),
                                            rec[:].unsqueeze(3).to_broadcast([P, 2, H, DH]),
                                            ALU.mult).then_inc(sem("att"), 1)
                if on["A"]:
                    pool.wait_ge(sem("qf"), done(t + 2))
                    pool.wait_ge(sem("stack0"), done(t + 1, SK))
                    pool.wait_ge(sem("stack1"), done(t + 1, SK))
                    hi(qp[0][:], qf[:]).then_inc(sem("qhi"), 1)
                    pool.wait_ge(sem("qhi"), done(t + 2))
                    lo(qp[1][:], qf[:], qp[0][:]).then_inc(sem("qsplit"), 1)
                if on["F"]:
                    pool.wait_ge(sem("var"), done(t - 2))
                    pool.wait_ge(sem("normed"), done(t - 3))
                    pool.sem_inc(sem("waited_pool"), 1)
                    nc.gpsimd.tensor_scalar(veps[:], mv[:, :, 1], 1.0, EPS, ALU.mult, ALU.add).then_inc(sem("veps"), 1)
                    pool.wait_ge(sem("veps"), done(t - 2))
                    nc.gpsimd.tensor_tensor(rstd[:], veps[:], mhalf[:], ALU.pow).then_inc(sem("rstd"), 1)
                if on["C"]:
                    pool.wait_ge(sem("eself"), done(t))
                    pool.wait_ge(sem("vself"), done(t))
                    pool.wait_ge(sem("nv"), done(t - 2, 2))
                    nc.gpsimd.tensor_tensor(tv[par][:].rearrange("p c (h d) -> p c h d", d=DH),
                                            vself[:].rearrange("p c (h d) -> p c h d", d=DH),
                                            eself[par][:].unsqueeze(3).to_broadcast([P, 2, H, DH]),
                                            ALU.mult).then_inc(sem("tv"), 1)
                if on["A"]:
                    pool.wait_ge(sem("kf"), done(t + 2))
                    hi(kp[0][:], kf[:]).then_inc(sem("khi"), 1)
                if on["F"]:
                    pool.wait_ge(sem("normed"), done(t - 2))
                    pool.wait_ge(sem("ld_ga"), done(t - 2, 16))
                    nc.gpsimd.tensor_tensor(yg[:], yn[:], gar[:].unsqueeze(1).to_broadcast([P, 2, D]),
                                            ALU.mult).then_inc(sem("gained"), 1)
                if on["A"]:
                    pool.wait_ge(sem("khi"), done(t + 2))
                    lo(kp[1][:], kf[:], kp[0][:]).then_inc(sem("ksplit"), 1)
                if on["E"]:
                    pool.wait_ge(sem("ld_xr"), done(t - 1, 16))
                    nc.gpsimd.tensor_tensor(xb[:], xr[:], bop[:].unsqueeze(1).to_broadcast([P, 2, D]),
                                            ALU.add).then_inc(sem("xb"), 1)
                    pool.wait_ge(sem("ld_wad"), done(t - 1, 16))
                    pool.wait_ge(sem("h_pe"), done(t - 2))
                    pool.wait_ge(sem("ad_pe"), done(t - 2))
                    twice = w1raw.unsqueeze(2).to_broadcast([P, NC2, 2, A1])
                    hi(w1p[0][:], twice).then_inc(sem("whi"), 1)
                    hi(w2p[0][:], w2raw).then_inc(sem("whi"), 1)
                    pool.wait_ge(sem("whi"), done(t - 1, 2))
                    lo(w1p[1][:], twice, w1p[0][:]).then_inc(sem("wlo"), 1)
                    lo(w2p[1][:], w2raw, w2p[0][:]).then_inc(sem("wsplit"), 1)
                    pool.wait_ge(sem("x1"), done(t - 1))
                    pool.wait_ge(sem("ld_b"), done(t - 1, 32))
                    pool.wait_ge(sem("y"), done(t - 2))
                    nc.gpsimd.tensor_tensor(x1b2[:], x1[:], b2r[:].unsqueeze(1).to_broadcast([P, 2, D]),
                                            ALU.add).then_inc(sem("x1b2"), 1)
                    pool.wait_ge(sem("x2"), done(t - 2))
                    nc.gpsimd.tensor_tensor(x1be[:], x1[:], ber[:].unsqueeze(1).to_broadcast([P, 2, D]),
                                            ALU.add).then_inc(sem("x1sum"), 1)

            pool.wait_ge(ld_w, 16 * WL)
            for j in range(SUBJ):
                if j == 2:
                    pool.wait_ge(ready, 1)
                    step(-2, 0)
                i = j % NCAT
                pool.wait_ge(ld_lc[i], 16 * (j // NCAT + 1))
                nc.gpsimd.tensor_tensor(lcat[i][:, :, 0:D], lcat[i][:, :, 0:D], eye2[:], ALU.add).then_inc(eyec, 1)
            steps(pool, step)

        @block.scalar
        def _(act):
            def copy(dst, src, bias=0.0):
                return nc.scalar.activation(dst, src, ACT.Identity, bias=bias)

            def halves(name):
                return bank[name][:].rearrange("p (c q) -> p c q", c=2)

            def step(t, par):
                on = at_work(t)
                odd = 1 - par

                def unit(s):
                    if not on["C"]:
                        return
                    g, kb = s // 4, s % 2
                    act.wait_ge(sem("st_ready"), before(t, s + 1))
                    if s % 4 == 0:
                        act.wait_ge(sem("pv_done"), max(0, 4 * t + g - 1) if isinstance(t, int) else 4 * t + g - 1)
                    nc.scalar.activation(pt[:, g % 2, kb, 2 * (s // 2 % 2):2 * (s // 2 % 2) + 2, :],
                                         ST[s % 2][:].rearrange("p (h q) -> p h q", h=2), ACT.Exp,
                                         scale=SCALE).then_inc(sem("exp_done"), 1)

                def groups(b, k):
                    act.wait_ge(sem("pv_done"), done(b, 4, 2 * k + 2))
                    act.wait_ge(sem("num_pe"), done(b - 1, 2))
                    copy(pvt[:, 2 * k:2 * k + 2, :], PV[:].rearrange("p (g q) -> p g q", g=2)).then_inc(sem("pvt"), 1)

                unit(0)
                if on["A"]:
                    act.wait_ge(sem(f"ld_xs{par}"), loaded(t + 2, par))
                    act.wait_ge(sem("vs_pe"), done(t))
                    copy(ss[par][0][:], sin[par]).then_inc(sem("shi"), 1)
                if on["C"]:
                    act.wait_ge(sem("m1_pe"), done(t))
                    act.wait_ge(sem("mput0"), done(t, 16))
                    copy(mrow[:], bank["m1"][0:PAIRS, 0:S].rearrange("p (c q) -> p c q", c=2)).then_inc(sem("mrow1"), 1)
                    act.wait_ge(sem("earg"), done(t))
                    act.wait_ge(sem("tv"), done(t - 2))
                    act.wait_ge(sem("tot"), done(t - 2, 2))
                    nc.scalar.activation(eself[par][:], earg[:], ACT.Exp, scale=SCALE).then_inc(sem("eself"), 1)
                unit(1)
                if on["E"]:
                    groups(t - 1, 1)
                if on["G"]:
                    act.wait_ge(sem("x3"), done(t - 3, 2))
                    act.wait_ge(sem("tvv"), done(t - 4))
                    nc.scalar.activation(th[:], x3[:, :, D:NX], ACT.Tanh).then_inc(sem("tanh"), 1)
                unit(2)
                if on["F"]:
                    act.wait_ge(sem("h_pe"), done(t - 2))
                    act.wait_ge(sem("ad_pe"), done(t - 3))
                    act.wait_ge(sem("ld_wad"), done(t - 2, 16))
                    nc.scalar.activation(hst[:], bank["h"][:, 0:S], ACT.Relu, bias=b1c[:, 0:1]).then_inc(sem("hhi"), 1)
                if on["A"]:
                    act.wait_ge(sem(f"ld_xs{par}"), loaded(t + 2, par))
                    act.wait_ge(sem("v_pe"), done(t))
                    copy(xs[par][0][:], xin[par]).then_inc(sem("xhi"), 1)
                unit(3)
                if on["A"]:
                    act.wait_ge(sem("q_pe"), done(t + 2))
                    act.wait_ge(sem("qsplit"), done(t + 1))
                    act.wait_ge(sem("prod"), done(t + 1))
                    for e in range(2):
                        copy(qf[:, e, :], bank["q"][:, e * S:e * S + S], bqc[:, e:e + 1]).then_inc(sem("qe" if e == 0 else "qf"), 1)
                unit(4)
                unit(5)
                if on["G"]:
                    act.wait_ge(sem("nm3"), done(t - 3))
                    act.wait_ge(sem("pT_pe"), done(t - 4))
                    act.wait_ge(sem("r3"), done(t - 4))
                    for i in range(2):
                        nc.scalar.activation(pe3[:, i, :], msc[:, i, :], ACT.Exp, bias=nm3[:, i:i + 1],
                                             accum_out=sum3[:, i:i + 1]).then_inc(sem("pe3"), 1)
                unit(6)
                unit(7)
                if on["A"]:
                    act.wait_ge(sem("k_pe"), done(t + 2))
                    act.wait_ge(sem("ksplit"), done(t + 1))
                    for e in range(2):
                        copy(kf[:, e, :], bank["k"][:, e * S:e * S + S], bkc[:, e:e + 1]).then_inc(sem("ke" if e == 0 else "kf"), 1)
                unit(8)
                if on["G"]:
                    act.wait_ge(sem("pT_pe"), done(t - 3))
                    act.wait_ge(sem("pool_pe"), done(t - 4))
                    copy(p3T[:], halves("pT")).then_inc(sem("p3T"), 1)
                unit(9)
                if on["B"]:
                    act.wait_ge(sem("v_pe"), done(t + 1))
                    act.wait_ge(sem("pv_done"), done(t - 1, 4))
                    copy(vaug[odd][:, :, :, 0:DH],
                         bank["v"][:].rearrange("p (c h d) -> p c h d", c=2, d=DH)).then_inc(sem("v"), 1)
                if on["E"]:
                    act.wait_ge(sem("aT_pe"), done(t - 1))
                    act.wait_ge(sem("wo_pe"), done(t - 2))
                    copy(aT[0][:], halves("aT")).then_inc(sem("aThi"), 1)
                unit(10)
                if on["C"]:
                    groups(t, 0)
                unit(11)
                if on["F"]:
                    act.wait_ge(sem("x2T_pe"), done(t - 2))
                    act.wait_ge(sem("lin"), done(t - 3, 2))
                    copy(x2T[0][:], halves("x2T")).then_inc(sem("x2Thi"), 1)
                if on["B"]:
                    act.wait_ge(sem("m0_pe"), done(t + 1))
                    act.wait_ge(sem("mput1"), done(t, 16))
                    copy(mrow[:], bank["m0"][0:PAIRS, 0:S].rearrange("p (c q) -> p c q", c=2)).then_inc(sem("mrow0"), 1)
                unit(12)
                unit(13)
                if on["B"]:
                    act.wait_ge(sem("vs_pe"), done(t + 1))
                    act.wait_ge(sem("tv"), done(t))
                    copy(vself[:], halves("vs")).then_inc(sem("vself"), 1)
                unit(14)
                if on["E"]:
                    act.wait_ge(sem("x1T_pe"), done(t - 1))
                    act.wait_ge(sem("h_pe"), done(t - 2))
                    copy(x1T[0][:], halves("x1T")).then_inc(sem("x1Thi"), 1)
                unit(15)

            for j in range(SUBJ):
                i = j % 2
                if j == 2:
                    act.wait_ge(ready, 1)
                    step(-2, 0)
                act.wait_ge(fold, j + 1)
                if j >= 2:
                    act.wait_ge(lsplit, j - 1)
                    act.wait_ge(lsaved[i], 16 * (j // 2))
                if j == 0:
                    act.wait_ge(ready, 1)
                m = lcat[j % NCAT]
                copy(m[:, :, D:NX], SN[i][:, 0:2 * A1].rearrange("p (c n) -> p c n", c=NC2)).then_inc(cat, 1)
                act.wait_ge(cat, j + 1)
                act.wait_ge(eyec, j + 1)
                copy(lwst[i][:, 0], m).then_inc(lhi, 1)
            steps(act, step)

        @block.vector
        def _(dve):
            def wide(n):
                return bank[n][:].rearrange("p (c q) -> p c q", c=2)

            link = sem("set_dve_order")
            n_link = [0]

            def after(ins):
                n_link[0] += 1
                ins.then_inc(link, 1)
                dve.wait_ge(link, n_link[0])

            nc.vector.memset(qst[0][0:96].bitcast(F32), 0.0).then_inc(link, 1)
            for i in range(2):
                nc.vector.memset(vaug[i][:, :, :, DH + 1:VW], 0.0).then_inc(link, 1)
                nc.vector.memset(vaug[i][:, :, :, DH:DH + 1], 1.0).then_inc(link, 1)
            n_link[0] += 5
            dve.wait_ge(link, n_link[0])
            dve.wait_ge(ld_w, 16 * WL)
            after(nc.vector.tensor_copy(lenf[:], leni[:]))
            nc.vector.tensor_scalar(mrows, kid, lenf[:, 0:1], NEG, ALU.is_ge, ALU.mult).then_inc(sem("mask_split"), 1)
            for n in ("q", "k", "v", "o"):
                after(nc.vector.tensor_copy(W[n][0][:], raw[n]))
                after(nc.vector.tensor_tensor(W[n][1][:], raw[n], W[n][0][:].bitcast(F32), ALU.subtract))
            after(nc.vector.tensor_copy(headsr[:], heads[:]))
            for c in range(NC2):
                nc.vector.tensor_copy(bvb[:, c, :], bcol[:, 8 + c:9 + c].to_broadcast([P, P])).then_inc(set_dve, 1)
            dve.wait_ge(set_pe, 1)
            bias = M[0]
            after(nc.vector.tensor_tensor(bqc[:], bias[:, 0:2], bcol[:, 0:2], ALU.add))
            after(nc.vector.tensor_tensor(bkc[:], bias[:, 2:4], bcol[:, 2:4], ALU.add))
            after(nc.vector.tensor_tensor(bsc[:], bias[:, 4:6], bcol[:, 2:4], ALU.add))
            after(nc.vector.tensor_tensor(bop[:], M[1][:, 0:D], bos, ALU.add))
            nc.vector.tensor_tensor(btab[:, D:NX], M[2][0:SUBJ, 0:A1], b3s, ALU.add).then_inc(sem("btab"), 1)
            nc.vector.memset(rec[:], 0.0).then_inc(link, 1)
            n_link[0] += 1
            dve.wait_ge(link, n_link[0])
            dve.wait_ge(sem("btab"), 1)
            dve.sem_inc(ready, 1)

            def eye(j):
                dve.wait_ge(ld_ln[j % 2], 16 * (j // 2 + 1))
                nc.vector.tensor_tensor(lwn[j % 2], lwn[j % 2], eye2[:], ALU.add).then_inc(eyed, 1)

            eye(0)
            for j in range(SUBJ):
                i = j % 2
                if j + 1 < SUBJ:
                    eye(j + 1)
                dve.wait_ge(lhi, j + 1)
                nc.vector.tensor_tensor(lwst[i][:, 1], lcat[j % NCAT], lwst[i][:, 0].bitcast(F32),
                                        ALU.subtract).then_inc(lsplit, 1)
            for i in range(2):
                dve.wait_ge(lsaved[i], 16 * SUBJ // 2)
            dve.wait_ge(saved, 32)
            nc.vector.memset(kst[1][96:98].bitcast(F32), 1.0).then_inc(tables, 1)
            dve.wait_ge(tables, 1)
            dve.wait_ge(sem("ld_v3"), 32)

            def step(t, par):
                on = at_work(t)
                odd = 1 - par

                def maxima(half, b, i):
                    hs = slice(8 * half, 8 * half + 8)
                    dve.wait_ge(sem("nself"), done(b))
                    dve.wait_ge(sem("maxed"), before(b, 8 * half + 8))
                    dve.wait_ge(sem(f"m{half}_pe"), done(b - 2))
                    return nc.vector.scalar_tensor_tensor(out=mneg[i][:, :, hs], in0=mx[i][:, :, hs], scalar=-1.0,
                                                          in1=nself[i][:, :, hs], op0=ALU.mult, op1=ALU.min)

                def unit(s):
                    if not on["B"]:
                        return
                    dve.wait_ge(sem("sn_ready"), before(t + 1, s + 1))
                    if s < 2:
                        dve.wait_ge(sem("earg"), done(t - 1))
                    nc.vector.tensor_reduce(out=mx[odd][:, s % 2, 2 * (s // 2):2 * (s // 2) + 2],
                                            in_=SN[s % 2][:].rearrange("p (h k) -> p h k", h=2),
                                            op=ALU.max, axis=AX.X).then_inc(sem("maxed"), 1)

                def low(dst, name, high):
                    return nc.vector.tensor_tensor(dst[:], wide(name), high[:].bitcast(F32), ALU.subtract)

                def numerators(i):
                    v4 = bank[f"num{i}"][:].rearrange("p (h w) -> p h w", w=VW)
                    dve.wait_ge(sem("num_pe"), done(t - 1, 2, i + 1))
                    dve.wait_ge(sem("eself"), done(t - 1))
                    dve.wait_ge(sem("tv"), done(t - 1))
                    dve.wait_ge(sem("aT_pe"), done(t - 2))
                    nc.vector.tensor_tensor(tot[:, i, :], v4[:, :, DH], eself[odd][:, i, :],
                                            ALU.add).then_inc(sem("tot"), 1)
                    nc.vector.tensor_tensor(nv[:, i, :].rearrange("p (h d) -> p h d", d=DH), v4[:, :, 0:DH],
                                            tv[odd][:, i, :].rearrange("p (h d) -> p h d", d=DH),
                                            ALU.add).then_inc(sem("nv"), 1)
                    dve.wait_ge(sem("tot"), done(t - 1, 2, i + 1))
                    nc.vector.reciprocal(rec[:, i, :], tot[:, i, :]).then_inc(sem("rec"), 1)

                def third(i, b):
                    dve.wait_ge(sem("lin"), done(b, 2, i + 1))
                    dve.wait_ge(sem("ld_lb"), done(b, 16))
                    dve.wait_ge(sem("tanh"), done(b - 1))
                    dve.wait_ge(sem("pool_pe"), done(b - 1))
                    dve.wait_ge(sem("outs"), done(b - 1, 2))
                    nc.vector.tensor_tensor(x3[:, i, :], bank[f"lin{i}"][:, 0:NX], lbr[:],
                                            ALU.add).then_inc(sem("x3"), 1)

                if on["C"]:
                    maxima(1, t, par).then_inc(sem("mneg1"), 1)
                    dve.wait_ge(sem("mneg1"), done(t))
                    dve.wait_ge(sem("mneg0"), done(t))
                    dve.wait_ge(sem("eself"), done(t - 1))
                    nc.vector.tensor_tensor(earg[:], mneg[par][:].bitcast(F32), nself[par][:],
                                            ALU.subtract).then_inc(sem("earg"), 1)
                unit(0)
                if on["G"]:
                    third(1, t - 3)
                unit(1)
                if on["B"]:
                    dve.wait_ge(sem("ks_pe"), done(t + 1))
                    dve.wait_ge(sem("qf"), done(t + 1))
                    dve.wait_ge(sem("qe"), done(t + 1))
                    dve.wait_ge(sem("psplit"), done(t))
                    for e in range(2):
                        nc.vector.scalar_tensor_tensor(out=pr[:, e, :], in0=bank["ks"][:, e * S:e * S + S],
                                                       scalar=bsc[:, e:e + 1], in1=qf[:, e, :], op0=ALU.add,
                                                       op1=ALU.mult).then_inc(sem("pr0" if e == 0 else "prod"), 1)
                unit(2)
                if on["G"]:
                    dve.wait_ge(sem("tanh"), done(t - 3))
                    dve.wait_ge(sem("sc"), done(t - 4))
                    nc.vector.tensor_tensor(tvv[:], th[:], v3r[:], ALU.mult).then_inc(sem("tvv"), 1)
                    dve.wait_ge(sem("tvv"), done(t - 3))
                    dve.wait_ge(sem("srep_pe"), done(t - 4))
                    nc.vector.tensor_reduce(out=sc[:], in_=tvv[:], op=ALU.add, axis=AX.X).then_inc(sem("sc"), 1)
                unit(3)
                if on["F"]:
                    dve.wait_ge(sem("hhi"), done(t - 2))
                    dve.wait_ge(sem("hlo"), done(t - 3))
                    nc.vector.tensor_scalar(hf[64:128, :], bank["h"][64:128, 0:S], b1c[64:128, 0:1], 0.0,
                                            ALU.add, ALU.max).then_inc(sem("hf"), 1)
                    dve.wait_ge(sem("hf"), done(t - 2))
                    nc.vector.tensor_tensor(hst[64:128, :], hf[64:128, :], hst[64:128, :].bitcast(F32),
                                            ALU.subtract).then_inc(sem("hlo"), 1)
                unit(4)
                if on["G"]:
                    dve.wait_ge(sem("srep_pe"), done(t - 3))
                    dve.wait_ge(sem("ld_pm"), done(t - 3, 16))
                    dve.wait_ge(sem("pe3"), done(t - 4, 2))
                    nc.vector.tensor_tensor(msc[:], bank["srep"][:, 0:S].unsqueeze(1).to_broadcast([P, 2, S]),
                                            pm[:, :, 0:S], ALU.add).then_inc(sem("masked"), 1)
                if on["E"]:
                    numerators(0)
                unit(5)
                if on["E"]:
                    numerators(1)
                if on["G"]:
                    dve.wait_ge(sem("masked"), done(t - 3))
                    nc.vector.tensor_reduce(out=nm3[:], in_=msc[:], op=ALU.max, axis=AX.X,
                                            negate=True).then_inc(sem("nm3"), 1)
                unit(6)
                if on["F"]:
                    dve.wait_ge(sem("ad_pe"), done(t - 2))
                    dve.wait_ge(sem("x1b2"), done(t - 2))
                    nc.vector.tensor_tensor(y[:], wide("ad"), x1b2[:], ALU.add).then_inc(sem("y"), 1)
                    dve.wait_ge(sem("y"), done(t - 2))
                    for i in range(2):
                        nc.vector.bn_stats(st[:, i, :], y[:, i, :]).then_inc(sem("st"), 1)
                    dve.wait_ge(sem("st"), done(t - 2, 2))
                    dve.wait_ge(sem("veps"), done(t - 3))
                    dve.sem_inc(sem("waited_dve"), 1)
                    nc.vector.bn_aggr(mv[:, 0, :], st[:, 0, :]).then_inc(sem("va"), 1)
                    nc.vector.bn_aggr(mv[:, 1, :], st[:, 1, :]).then_inc(sem("var"), 1)
                unit(7)
                unit(8)
                if on["B"]:
                    dve.wait_ge(sem("ss_pe"), done(t + 1))
                    dve.wait_ge(sem("earg"), done(t - 1))
                    nc.vector.tensor_scalar(nself[odd][:], bank["ss"][:, 0:2 * H].rearrange("p (c h) -> p c h", c=2),
                                            -1.0, None, ALU.mult).then_inc(sem("nself"), 1)
                if on["F"]:
                    dve.wait_ge(sem("rstd"), done(t - 2))
                    dve.wait_ge(sem("x2"), done(t - 3))
                    dve.wait_ge(sem("var"), done(t - 2))
                    dve.wait_ge(sem("va"), done(t - 2))
                    for i in range(2):
                        nc.vector.tensor_scalar(yn[:, i, :], y[:, i, :], mv[:, i, 0:1], rstd[:, i:i + 1],
                                                ALU.subtract, ALU.mult).then_inc(sem("norm0" if i == 0 else "normed"), 1)
                if on["G"]:
                    dve.wait_ge(sem("pe3"), done(t - 3, 2))
                    dve.wait_ge(sem("outs"), done(t - 4, 2))
                    nc.vector.tensor_tensor(sc3[:], sum3[:], pm[:, :, S], ALU.mult).then_inc(sem("sc3"), 1)
                    dve.wait_ge(sem("sc3"), done(t - 3))
                    nc.vector.reciprocal(r3[:], sc3[:]).then_inc(sem("r3"), 1)
                unit(9)
                if on["B"]:
                    maxima(0, t + 1, odd).then_inc(sem("mneg0"), 1)
                unit(10)
                if on["E"]:
                    dve.wait_ge(sem("aThi"), done(t - 1))
                    dve.wait_ge(sem("wo_pe"), done(t - 2))
                    low(aT[1], "aT", aT[0]).then_inc(sem("aTlo"), 1)
                if on["F"]:
                    dve.wait_ge(sem("gained"), done(t - 2))
                    dve.wait_ge(sem("x1sum"), done(t - 2))
                    dve.wait_ge(sem("x2T_pe"), done(t - 3))
                    nc.vector.tensor_tensor(x2[:], yg[:], x1be[:], ALU.add).then_inc(sem("x2"), 1)
                unit(11)
                unit(12)
                if on["F"]:
                    dve.wait_ge(sem("x2Thi"), done(t - 2))
                    dve.wait_ge(sem("lin"), done(t - 3, 2))
                    low(x2T[1], "x2T", x2T[0]).then_inc(sem("x2Tlo"), 1)
                if on["G"]:
                    dve.wait_ge(sem("pool_pe"), done(t - 3))
                    dve.wait_ge(sem("r3"), done(t - 3))
                    dve.wait_ge(sem("x3"), done(t - 3, 2))
                    dve.wait_ge(sem(f"stored{odd}"), loaded(t - 5, odd))
                    for i in range(2):
                        nc.vector.scalar_tensor_tensor(out=ob[odd][:, i, :], in0=bank["pool"][:, i * D:i * D + D],
                                                       scalar=r3[:, i:i + 1], in1=x3[:, i, 0:D], op0=ALU.mult,
                                                       op1=ALU.add).then_inc(sem("outs"), 1)
                unit(13)
                if on["E"]:
                    dve.wait_ge(sem("wo_pe"), done(t - 1))
                    dve.wait_ge(sem("xb"), done(t - 1))
                    dve.wait_ge(sem("x1T_pe"), done(t - 2))
                    dve.wait_ge(sem("x1sum"), done(t - 2))
                    dve.wait_ge(sem("x1b2"), done(t - 2))
                    nc.vector.tensor_tensor(x1[:], wide("wo"), xb[:], ALU.add).then_inc(sem("x1"), 1)
                unit(14)
                unit(15)
                if on["E"]:
                    dve.wait_ge(sem("x1Thi"), done(t - 1))
                    dve.wait_ge(sem("h_pe"), done(t - 2))
                    low(x1T[1], "x1T", x1T[0]).then_inc(sem("x1Tlo"), 1)
                if on["F"]:
                    third(0, t - 2)

            steps(dve, step)


def kernel(**a):
    import concourse.bacc as bacc
    from concourse.bass_utils import run_bass_kernel_spmd

    def c(v):
        return np.ascontiguousarray(v)

    order = np.array([(2 * (PH * half + p) + e) * DH + d
                      for e in range(2) for half in range(2) for d in range(DH) for p in range(PH)])
    ins = {n: np.asarray(v) for n, v in a.items()}
    col = lambda v: c(v.reshape(NC2, P).T)
    rows = np.arange(S)
    masks = np.stack([rows[None, :] <= rows[:, None], rows[None, :] >= rows[:, None], rows[None, :] != rows[:, None]])
    pmask = np.concatenate([np.where(masks, 0.0, NEG), masks.sum(-1, keepdims=True)], -1).astype(np.float32)
    heads = np.zeros((2 * P, H), np.float32)
    heads[np.arange(2 * P), order // DH] = 1.0
    wad = np.concatenate([ins["L1_cond_W1"].reshape(LANG, NC2, P, A1).transpose(0, 2, 1, 3).reshape(LANG, P, -1),
                          np.tile(ins["L1_cond_W2"], (1, 2, 1)), np.tile(ins["L1_cond_b1"], (1, 2))[:, :, None]], -1)
    data = {
        "x": c(ins["x"]), "xsT": np.stack([ins["x"].transpose(0, 2, 1), ins["fside_BxSxS_0"].transpose(0, 2, 1)], 1),
        "lens": c(ins["itok_B_18_1004"].reshape(B, 1)), "lang": c(ins["itok_B_0_8"].reshape(1, B)),
        "subj": c(ins["itok_B_0_7"].reshape(1, B)), "kind": c(ins["itok_B_0_2"].reshape(1, B)),
        "wq": c(ins["L0_cond_Wq"][:, order]), "bq": col(ins["L0_cond_bq"][order]),
        "wk": c(ins["L0_cond_Wk"][:, order]), "bk": col(ins["L0_cond_bk"][order]),
        "wv": c(ins["L0_cond_Wv"]), "bv": col(ins["L0_cond_bv"]),
        "wo": c(ins["L0_cond_Wo"]), "bo": c(ins["L0_cond_bo"].reshape(1, D)),
        "bprev": col(ins["L0_cond_b_prev"].reshape(-1)), "bself": col(ins["L0_cond_b_self"].reshape(-1)),
        "wad": wad, "b2": c(ins["L1_cond_b2"]),
        "gamma": c(ins["L1_cond_gamma"]), "beta": c(ins["L1_cond_beta"]),
        "lw": c(ins["L2_cond_weight"]), "lwT": c(ins["L2_cond_weight"].transpose(0, 2, 1)),
        "lb": c(ins["L2_cond_bias"]), "lbT": c(ins["L2_cond_bias"].T),
        "w3": c(ins["L3_cond_W1"]), "b3": c(ins["L3_cond_b1"].reshape(1, A1)), "v3": c(ins["L3_cond_v"].reshape(1, A1)),
        "ident": np.eye(P, dtype=np.float32), "eye2": np.eye(D, dtype=np.float32),
        "heads": c(heads.reshape(2, P, H).transpose(1, 0, 2)),
        "kidx": np.tile(np.arange(S, dtype=np.float32), (B, 1)), "pmask": pmask,
    }
    nc = bacc.Bacc("TRN2", target_bir_lowering=False, num_devices=1)
    aps = [nc.dram_tensor(f"in_{n}", v.shape, mybir.dt.from_np(v.dtype), kind="ExternalInput").ap()
           for n, v in data.items()]
    o = nc.dram_tensor("out_0", (B, S, D), F32, kind="ExternalOutput").ap()
    by = dict(zip(data, aps))
    block4(nc, by["x"], by["xsT"], by["lens"], by["lang"], by["subj"], by["kind"], by["wq"], by["bq"],
           by["wk"], by["bk"], by["wv"], by["bv"], by["wo"], by["bo"], by["bprev"], by["bself"], by["wad"],
           by["b2"], by["gamma"], by["beta"], by["lw"], by["lwT"], by["lb"], by["lbT"], by["w3"], by["b3"],
           by["v3"], by["ident"], by["eye2"], by["heads"], by["kidx"], by["pmask"], o)
    r = run_bass_kernel_spmd(nc, [{f"in_{n}": v for n, v in data.items()}], core_ids=[0])
    return r.results[0]["out_0"]
```
